# Optimizing a Trainium2 kernel written in Bass

```python
import numpy as np
import jax
import jax.numpy as jnp

def _softmax(x, axis=-1):
    return jax.nn.softmax(x, axis=axis)

def _gelu(x):
    return jax.nn.gelu(x, approximate=True)

def _silu(x):
    return jax.nn.silu(x)

def _sigmoid(x):
    return jax.nn.sigmoid(x)

def _layernorm(x, axis=-1, eps=1e-05):
    m = jnp.mean(x, axis=axis, keepdims=True)
    v = jnp.var(x, axis=axis, keepdims=True)
    return (x - m) / jnp.sqrt(v + eps)

def _scatter_add(tgt, idx, src, axis=0):
    return tgt.at[idx].add(src)

def _segment_sum(src, seg, n):
    return jax.ops.segment_sum(src, seg, n)
kernel_name = 'mk_gnn_preln_d1_gnn_r8_5211be'

def setup_inputs(seed: int=0):
    np.random.seed(seed)
    _w = jnp.asarray

    def _rec_inputs():
        import jax
        import jax.numpy as jnp
        _gk = jax.random.key(seed)
        x = -0.000202 + 1 * jax.random.normal(jax.random.fold_in(_gk, 1), (12500, 64), jnp.float32)
        src = jax.random.randint(jax.random.fold_in(_gk, 2), (400000,), 0, 12500, jnp.int32)
        dst = jax.random.randint(jax.random.fold_in(_gk, 3), (400000,), 0, 12500, jnp.int32)
        _o = jnp.argsort(dst, stable=True)
        src = src[_o]
        dst = dst[_o]
        edge_weight1 = 9.9816e-05 + 0.999782 * jax.random.normal(jax.random.fold_in(_gk, 12), (400000, 1), jnp.float32)
        return (x, src, dst, edge_weight1)
    x, src, dst, edge_weight1 = _rec_inputs()

    def _L0_gnn_setup():
        import jax, jax.numpy as jnp
        import numpy as np
        N = 12500
        E = 156250
        H = 64
        T = 2

        def _gru_cell(inp, h, Wih, bih, Whh, bhh):
            gi = inp @ Wih.T + bih
            gh = h @ Whh.T + bhh
            i_r, i_z, i_n = jnp.split(gi, 3, axis=1)
            h_r, h_z, h_n = jnp.split(gh, 3, axis=1)
            r = jax.nn.sigmoid(i_r + h_r)
            z = jax.nn.sigmoid(i_z + h_z)
            n = jnp.tanh(i_n + r * h_n)
            return (1.0 - z) * n + z * h
        key = jax.random.key(seed)
        ks = jax.random.split(key, 10)
        s = 0.1
        return {'x': jax.random.normal(ks[0], (N, H), dtype=jnp.float32), 'edge_index': jax.random.randint(ks[1], (2, E), 0, N, dtype=jnp.int64), 'edge_attr': jax.random.normal(ks[2], (E, 1), dtype=jnp.float32), 'msg_W': jax.random.normal(ks[3], (T, H, 2 * H + 1), dtype=jnp.float32) * s, 'msg_b': jax.random.normal(ks[4], (T, H), dtype=jnp.float32) * s, 'gru_Wih': jax.random.normal(ks[5], (T, 3 * H, H), dtype=jnp.float32) * s, 'gru_bih': jax.random.normal(ks[6], (T, 3 * H), dtype=jnp.float32) * s, 'gru_Whh': jax.random.normal(ks[7], (T, 3 * H, H), dtype=jnp.float32) * s, 'gru_bhh': jax.random.normal(ks[8], (T, 3 * H), dtype=jnp.float32) * s}
    _L0_gnn_all = _L0_gnn_setup()
    _L0_gnn_in = {k: v for k, v in _L0_gnn_all.items() if k in ('msg_W', 'msg_b', 'gru_Wih', 'gru_bih', 'gru_Whh', 'gru_bhh')}
    del _L0_gnn_all
    return {'x': x, 'src': src, 'dst': dst, 'edge_weight1': edge_weight1, 'L0_gnn_msg_W': _L0_gnn_in['msg_W'], 'L0_gnn_msg_b': _L0_gnn_in['msg_b'], 'L0_gnn_gru_Wih': _L0_gnn_in['gru_Wih'], 'L0_gnn_gru_bih': _L0_gnn_in['gru_bih'], 'L0_gnn_gru_Whh': _L0_gnn_in['gru_Whh'], 'L0_gnn_gru_bhh': _L0_gnn_in['gru_bhh']}

def reference(x, src, dst, edge_weight1, L0_gnn_msg_W, L0_gnn_msg_b, L0_gnn_gru_Wih, L0_gnn_gru_bih, L0_gnn_gru_Whh, L0_gnn_gru_bhh):
    import jax
    import jax.numpy as jnp

    def _L0_gnn_ref(x, edge_index, edge_attr, msg_W, msg_b, gru_Wih, gru_bih, gru_Whh, gru_bhh):
        import jax, jax.numpy as jnp
        import numpy as np
        N = 12500
        E = 156250
        H = 64
        T = 2

        def _gru_cell(inp, h, Wih, bih, Whh, bhh):
            gi = inp @ Wih.T + bih
            gh = h @ Whh.T + bhh
            i_r, i_z, i_n = jnp.split(gi, 3, axis=1)
            h_r, h_z, h_n = jnp.split(gh, 3, axis=1)
            r = jax.nn.sigmoid(i_r + h_r)
            z = jax.nn.sigmoid(i_z + h_z)
            n = jnp.tanh(i_n + r * h_n)
            return (1.0 - z) * n + z * h
        row, col = (edge_index[0], edge_index[1])
        num_rounds = msg_W.shape[0]
        for t in range(num_rounds):
            src = x[row]
            dest = x[col]
            m_input = jnp.concatenate([dest, src, edge_attr], axis=1)
            messages = m_input @ msg_W[t].T + msg_b[t]
            agg = jax.ops.segment_sum(messages, row, num_segments=x.shape[0])
            x = _gru_cell(agg, x, gru_Wih[t], gru_bih[t], gru_Whh[t], gru_bhh[t])
        return x
    edge_index = jnp.stack([src, dst])
    h = jnp.maximum(_layernorm(x, axis=-1), 0.0)
    x = x + _L0_gnn_ref(h, edge_index, edge_weight1, L0_gnn_msg_W, L0_gnn_msg_b, L0_gnn_gru_Wih, L0_gnn_gru_bih, L0_gnn_gru_Whh, L0_gnn_gru_bhh)
    return x

_drawn_inputs = setup_inputs


def setup_inputs(seed=0):
    import zlib

    import numpy as np

    out = dict(_drawn_inputs(seed))
    spreads = {}
    factors = {}
    for name, (base, spread) in spreads.items():
        noise = np.random.default_rng([zlib.crc32(name.encode()), seed]).standard_normal(out[name].shape)
        drawn = base * np.exp(spread * noise) if base else spread * noise
        out[name] = jnp.asarray(drawn.astype(out[name].dtype))
    for name, factor in factors.items():
        out[name] = (out[name] * factor).astype(out[name].dtype)
    return out
```

```python
from contextlib import ExitStack

import concourse.bass as bass
from concourse import mybir

P = 128
F32 = mybir.dt.float32
I32 = mybir.dt.int32
ALU = mybir.AluOpType
ACT = mybir.ActivationFunctionType
AX = mybir.AxisListType
EPS = 1e-5


class Chain:

    def __init__(self, engine, sem):
        self.engine, self.sem, self.at = engine, sem, 0

    def __call__(self, ins):
        self.at += 1
        ins.then_inc(self.sem, 1)
        self.engine.wait_ge(self.sem, self.at)


def build(nc, x, src, dst, attr, msg_W, msg_b, Wih, bih, Whh, bhh, out):
    N, H = x.shape
    E = src.shape[0]
    ROUNDS = msg_W.shape[0]
    NT = -(-N // P)
    NP = NT * P
    TAIL = N - (NT - 1) * P
    ET = E // P
    assert E % P == 0 and H == 64 and NT % 2 == 0
    HA = H + 2
    G = 3 * H
    SKIP = float(1 << 22)

    with ExitStack() as ctx:
        def sb(name, shape, dt=F32):
            return ctx.enter_context(nc.sbuf_tensor(name, shape, dt))

        def ps(name, shape, dt=F32):
            return ctx.enter_context(nc.psum_tensor(name, shape, dt))

        def sem(name):
            return ctx.enter_context(nc.semaphore(name))

        h_dram = nc.dram_tensor("h_dram", [NP, H], F32, kind="Internal").ap()
        sums_dram = nc.dram_tensor("sums_dram", [NP, HA], F32, kind="Internal").ap()

        h = sb("h", [P, NT, HA])
        wide = sb("wide", [P, NT, H])
        total, mean, var, std, newton, rstd = [sb(n, [P, NT]) for n in ("total", "mean", "var", "std", "newton", "rstd")]
        ident = sb("ident", [P, P])
        earlier = sb("earlier", [P, P])
        ones = sb("ones", [P, P])
        zeros = sb("zeros", [P, HA])
        wmsg = sb("wmsg", [H, ROUNDS, 2 * H + 2])
        wih = sb("wih", [H, 3, ROUNDS, H])
        whh = sb("whh", [H, 3, ROUNDS, H])
        wihT = sb("wihT", [H, ROUNDS, G])
        pick = sb("pick", [HA, 2])
        w_sum = sb("w_sum", [H, ROUNDS, G])
        w_node = sb("w_node", [HA, ROUNDS, 4 * H + G])
        bias = sb("bias", [HA, ROUNDS, 4 * H])

        src_sb = sb("src_sb", [P, ET], I32)
        dst_sb = sb("dst_sb", [P, ET], I32)
        attr_sb = sb("attr_sb", [P, ET])
        src_now = sb("src_now", [P, 1], I32)
        dst_now = sb("dst_now", [P, 1], I32)
        put_at = sb("put_at", [P, 1], I32)
        srcf = sb("srcf", [P, 1])
        payload = sb("payload", [P, HA])
        before = sb("before", [P, HA])
        after = sb("after", [P, HA])
        same = sb("same", [P, P])
        dup = sb("dup", [P, P])
        ndup = sb("ndup", [P, 1])
        putf = sb("putf", [P, 1])

        sums = [sb(f"sums{b}", [P, HA]) for b in range(2)]
        hcur = [sb(f"hcur{b}", [P, HA]) for b in range(2)]
        sumT = [sb(f"sumT{b}", [H, P]) for b in range(2)]
        hT = [sb(f"hT{b}", [HA, P]) for b in range(2)]
        gi = [sb(f"gi{b}", [P, G]) for b in range(2)]
        rz = [sb(f"rz{b}", [P, 2 * H]) for b in range(2)]
        tn = [sb(f"tn{b}", [P, H]) for b in range(2)]
        cand = [sb(f"cand{b}", [P, H]) for b in range(2)]

        ps_a = ps("ps_a", [P, 512])
        ps_b = ps("ps_b", [P, 512])
        ps_T = ps("ps_T", [P, 2 * P])
        ps_gates = [ps(f"ps_gates{b}", [P, 512]) for b in range(2)]

        padded = sem("padded")
        const = sem("const")
        inputs = sem("inputs")
        cleared = sem("cleared")
        var_ready = sem("var_ready")
        std_ready = sem("std_ready")
        turned = sem("turned")
        gate_w = sem("gate_w")
        biases = sem("biases")
        folded = sem("folded")
        fold_used = sem("fold_used")
        dve_own = sem("dve_own")
        N_CONST, N_INPUTS, N_BIASES = 6, 16 * (7 + 2 * ROUNDS), 16 * 3 * ROUNDS

        with nc.Block() as block:
            @block.sync
            def _(sp):
                with nc.allow_non_contiguous_dma(reason="small weights"):
                    sp.wait_ge(padded, 1)
                    sp.dma_start(h[:, 0:NT - 1, 0:H],
                                 x[0:(NT - 1) * P, :].rearrange("(t p) f -> p t f", p=P)).then_inc(inputs, 16)
                    sp.dma_start(h[0:TAIL, NT - 1, 0:H], x[(NT - 1) * P:N, :]).then_inc(inputs, 16)
                    sp.dma_start(src_sb[:], src.rearrange("(p t) -> p t", p=P)).then_inc(inputs, 16)
                    sp.dma_start(dst_sb[:], dst.rearrange("(p t) -> p t", p=P)).then_inc(inputs, 16)
                    sp.dma_start(attr_sb[:], attr.rearrange("(p t) o -> p (t o)", p=P)).then_inc(inputs, 16)
                    sp.dma_start(wmsg[:, :, 0:2 * H + 1], msg_W.rearrange("r m k -> m r k")).then_inc(inputs, 16)
                    sp.dma_start(wmsg[:, :, 2 * H + 1:2 * H + 2],
                                 msg_b.rearrange("r (m o) -> m r o", o=1)).then_inc(inputs, 16)
                    for r in range(ROUNDS):
                        sp.dma_start(wih[:, :, r, :], Wih[r].rearrange("(g m) k -> m g k", g=3)).then_inc(inputs, 16)
                        sp.dma_start(whh[:, :, r, :], Whh[r].rearrange("(g m) k -> m g k", g=3)).then_inc(inputs, 16)
                    sp.wait_ge(cleared, 2)
                    for r in range(ROUNDS):
                        sp.dma_start(w_node[HA - 1:HA, r, 0:G], bih[r:r + 1, :]).then_inc(biases, 16)
                        sp.dma_start(bias[HA - 1:HA, r, 0:2 * H], bhh[r:r + 1, 0:2 * H]).then_inc(biases, 16)
                        sp.dma_start(bias[HA - 1:HA, r, 3 * H:4 * H], bhh[r:r + 1, 2 * H:G]).then_inc(biases, 16)

            @block.gpsimd
            def _(pool):
                nc.gpsimd.memset(h[:, NT - 1, 0:H], 0.0).then_inc(padded, 1)
                nc.gpsimd.memset(zeros[:], 0.0).then_inc(const, 1)
                nc.gpsimd.memset(ones[:], 1.0).then_inc(const, 1)
                pool.wait_ge(const, 2)
                nc.gpsimd.affine_select(out=ident[:], in_=ones[:], compare_op=ALU.is_equal, fill=0.0, base=0,
                                        pattern=[[-1, P]], channel_multiplier=1).then_inc(const, 1)
                nc.gpsimd.affine_select(out=earlier[:], in_=ones[:], compare_op=ALU.is_gt, fill=0.0, base=0,
                                        pattern=[[-1, P]], channel_multiplier=1).then_inc(const, 1)
                nc.gpsimd.affine_select(out=pick[:, 0:1], in_=ones[0:HA, 0:1], compare_op=ALU.is_equal, fill=0.0,
                                        base=-H, pattern=[[0, 1]], channel_multiplier=1).then_inc(const, 1)
                nc.gpsimd.affine_select(out=pick[:, 1:2], in_=ones[0:HA, 0:1], compare_op=ALU.not_equal, fill=0.0,
                                        base=-H, pattern=[[0, 1]], channel_multiplier=1).then_inc(const, 1)

            @block.tensor
            def _(te):
                te.wait_ge(inputs, N_INPUTS)
                te.wait_ge(const, N_CONST)
                for r in range(ROUNDS):
                    if r:
                        te.wait_ge(gate_w, 3 * r)
                    for g in range(3):
                        nc.tensor.transpose(ps_a[0:H, g * H:(g + 1) * H], wih[:, g, r, :], ident[0:H, 0:H])
                        last = nc.tensor.transpose(ps_b[0:H, g * H:(g + 1) * H], whh[:, g, r, :], ident[0:H, 0:H])
                    last.then_inc(turned, 1)
                te.wait_ge(gate_w, 3 * ROUNDS)
                for r in range(ROUNDS):
                    if r:
                        te.wait_ge(fold_used, 3 * r)
                    nc.tensor.matmul(ps_a[0:H, 0:G], wmsg[:, r, 0:H], wihT[:, r, :], start=True, stop=True)
                    nc.tensor.matmul(ps_b[0:HA, 0:G], wmsg[:, r, H:2 * H + 2], wihT[:, r, :], start=True,
                                     stop=True).then_inc(folded, 1)

            @block.scalar
            def _(act):
                act.wait_ge(var_ready, 1)
                nc.scalar.activation(std[:], var[:], ACT.Sqrt).then_inc(std_ready, 1)
                act.wait_ge(cleared, 2)
                for r in range(ROUNDS):
                    act.wait_ge(turned, r + 1)
                    nc.scalar.activation(wihT[:, r, :], ps_a[0:H, 0:G], ACT.Copy).then_inc(gate_w, 1)
                    nc.scalar.activation(w_node[0:H, r, 0:2 * H], ps_b[0:H, 0:2 * H], ACT.Copy).then_inc(gate_w, 1)
                    nc.scalar.activation(w_node[0:H, r, 3 * H:4 * H], ps_b[0:H, 2 * H:G], ACT.Copy).then_inc(gate_w, 1)

            @block.vector
            def _(dve):
                step = Chain(dve, dve_own)
                rows = h[:, :, 0:H]

                def per_row(t):
                    return t[:].rearrange("p (t o) -> p t o", o=1).broadcast_to([P, NT, H])

                nc.vector.memset(w_node[:], 0.0).then_inc(cleared, 1)
                nc.vector.memset(bias[:], 0.0).then_inc(cleared, 1)
                step(nc.vector.memset(h[:, :, H:H + 1], 0.0))
                step(nc.vector.memset(h[:, :, H + 1:HA], 1.0))
                dve.wait_ge(inputs, N_INPUTS)
                step(nc.vector.tensor_reduce(total[:], rows, AX.X, ALU.add))
                step(nc.vector.tensor_scalar(mean[:], total[:], 1.0 / H, None, ALU.mult))
                step(nc.vector.tensor_tensor(rows, rows, per_row(mean), ALU.subtract))
                step(nc.vector.tensor_tensor(wide[:], rows, rows, ALU.mult))
                step(nc.vector.tensor_reduce(total[:], wide[:], AX.X, ALU.add))
                nc.vector.tensor_scalar(var[:], total[:], 1.0 / H, EPS, ALU.mult, ALU.add).then_inc(var_ready, 1)
                dve.wait_ge(std_ready, 1)
                step(nc.vector.reciprocal(newton[:], std[:]))
                step(nc.vector.tensor_tensor(newton[:], newton[:], var[:], ALU.mult))
                step(nc.vector.tensor_tensor(newton[:], newton[:], std[:], ALU.add))
                step(nc.vector.tensor_scalar(newton[:], newton[:], 0.5, None, ALU.mult))
                step(nc.vector.reciprocal(rstd[:], newton[:]))
                step(nc.vector.tensor_tensor(rows, rows, per_row(rstd), ALU.mult))
                step(nc.vector.tensor_scalar(rows, rows, 0.0, None, ALU.max))
                dve.wait_ge(gate_w, 3 * ROUNDS)
                dve.wait_ge(biases, N_BIASES)
                for r in range(ROUNDS):
                    step(nc.vector.tensor_tensor(w_node[:, r, 0:4 * H], w_node[:, r, 0:4 * H], bias[:, r, :], ALU.add))
                    dve.wait_ge(folded, r + 1)
                    nc.vector.tensor_copy(w_sum[:, r, :], ps_a[0:H, 0:G]).then_inc(fold_used, 1)
                    nc.vector.scalar_tensor_tensor(out=w_node[:, r, 0:G], in0=ps_b[0:HA, 0:G], scalar=pick[:, 0:1],
                                                   in1=w_node[:, r, 0:G], op0=ALU.mult, op1=ALU.add).then_inc(fold_used, 1)
                    nc.vector.tensor_scalar(w_node[:, r, 4 * H:4 * H + G], ps_b[0:HA, 0:G], pick[:, 1:2], None,
                                            ALU.mult).then_inc(fold_used, 1)

        for r in range(ROUNDS):
            stored = sem(f"stored{r}")
            now_ready = sem(f"now_ready{r}")
            h_got = sem(f"h_got{r}")
            before_got = sem(f"before_got{r}")
            srcT_ready = sem(f"srcT_ready{r}")
            put_ready = sem(f"put_ready{r}")
            group_sum = sem(f"group_sum{r}")
            after_ready = sem(f"after_ready{r}")
            put_done = sem(f"put_done{r}")
            dve_edge = sem(f"dve_edge{r}")
            N_OWN = 6

            with nc.Block() as block:
                @block.sync
                def _(sp):
                    with nc.allow_non_contiguous_dma(reason="rows of nodes"):
                        sp.dma_start(h_dram.rearrange("(t p) f -> p t f", p=P), h[:, :, 0:H]).then_inc(stored, 16)
                        sp.dma_start(sums_dram.rearrange("(t p) f -> p t f", p=P),
                                     zeros[:].rearrange("p (o f) -> p o f", o=1).broadcast_to([P, NT, HA])).then_inc(stored, 16)
                    sp.wait_ge(stored, 32)

                @block.gpsimd
                def _(pool):
                    pool.wait_ge(stored, 32)
                    last_node = pool.to_reg(N - 1)
                    with pool.Fori(0, ET) as i:
                        pool.wait_ge(now_ready, 3 * i + 3)
                        nc.gpsimd.indirect_dma_start(
                            out=payload[:, 0:H], out_offset=None, in_=h_dram,
                            in_offset=bass.IndirectOffsetOnAxis(ap=dst_now[:], axis=0)).wait_op(stored, 32, 'sem-ge').then_inc(h_got, 16)
                        pool.wait_ge(put_done, 16 * i)
                        nc.gpsimd.indirect_dma_start(
                            out=before[:], out_offset=None, in_=sums_dram,
                            in_offset=bass.IndirectOffsetOnAxis(ap=src_now[:], axis=0)).wait_op(stored, 32, 'sem-ge').then_inc(before_got, 16)
                        pool.wait_ge(put_ready, i + 1)
                        pool.wait_ge(after_ready, i + 1)
                        nc.gpsimd.indirect_dma_start(
                            out=sums_dram, out_offset=bass.IndirectOffsetOnAxis(ap=put_at[:], axis=0),
                            in_=after[:], in_offset=None, bounds_check=last_node, oob_is_err=False).wait_op(stored, 32, 'sem-ge').then_inc(put_done, 16)
                    pool.wait_ge(put_done, 16 * ET)

                @block.tensor
                def _(te):
                    with te.Fori(0, ET) as i:
                        te.wait_ge(now_ready, 3 * i + 3)
                        nc.tensor.transpose(ps_a[:, 0:P], srcf[:].broadcast_to([P, P]), ident[:]).then_inc(srcT_ready, 1)
                        te.wait_ge(put_ready, i + 1)
                        te.wait_ge(h_got, 16 * i + 16)
                        nc.tensor.matmul(ps_b[:, 0:HA], same[:], payload[:], start=True, stop=True).then_inc(group_sum, 1)

                @block.vector
                def _(dve):
                    nc.vector.memset(payload[:, HA - 1:HA], 1.0)
                    with dve.Fori(0, ET) as i:
                        dve.wait_ge(put_done, 16 * i)
                        nc.vector.tensor_copy(dst_now[:], dst_sb[:, bass.ds(i, 1)]).then_inc(now_ready, 1)
                        nc.vector.tensor_copy(src_now[:], src_sb[:, bass.ds(i, 1)])
                        nc.vector.tensor_copy(payload[:, H:H + 1], attr_sb[:, bass.ds(i, 1)]).then_inc(now_ready, 1)
                        nc.vector.tensor_copy(srcf[:], src_sb[:, bass.ds(i, 1)]).then_inc(now_ready, 1)
                        dve.wait_ge(now_ready, 3 * i + 3)
                        dve.wait_ge(srcT_ready, i + 1)
                        nc.vector.tensor_scalar(same[:], ps_a[:, 0:P], srcf[:, 0:1], None, ALU.is_equal).then_inc(dve_edge, 1)
                        dve.wait_ge(dve_edge, N_OWN * i + 1)
                        nc.vector.tensor_tensor(dup[:], same[:], earlier[:], ALU.mult).then_inc(dve_edge, 1)
                        dve.wait_ge(dve_edge, N_OWN * i + 2)
                        nc.vector.tensor_reduce(ndup[:], dup[:], AX.X, ALU.add).then_inc(dve_edge, 1)
                        dve.wait_ge(dve_edge, N_OWN * i + 3)
                        nc.vector.tensor_scalar(ndup[:], ndup[:], 1.0, SKIP, ALU.min, ALU.mult).then_inc(dve_edge, 1)
                        dve.wait_ge(dve_edge, N_OWN * i + 4)
                        nc.vector.tensor_tensor(putf[:], ndup[:], srcf[:], ALU.add).then_inc(dve_edge, 1)
                        dve.wait_ge(dve_edge, N_OWN * i + 5)
                        nc.vector.tensor_copy(put_at[:], putf[:]).then_inc(put_ready, 1)
                        dve.wait_ge(group_sum, i + 1)
                        dve.wait_ge(before_got, 16 * i + 16)
                        nc.vector.tensor_tensor(after[:], before[:], ps_b[:, 0:HA], ALU.add).then_inc(after_ready, 1)
                        nc.vector.tensor_copy(ndup[:], ndup[:]).then_inc(dve_edge, 1)

            sums_got = [sem(f"sums_got{r}_{b}") for b in range(2)]
            cur_ready = sem(f"cur_ready{r}")
            T_turned = sem(f"T_turned{r}")
            T_ready = sem(f"T_ready{r}")
            gates_ready = sem(f"gates_ready{r}")
            gi_ready = sem(f"gi_ready{r}")
            rz_ready = sem(f"rz_ready{r}")
            tn_ready = sem(f"tn_ready{r}")
            cand_ready = sem(f"cand_ready{r}")
            h_new = sem(f"h_new{r}")
            dve_gru = sem(f"dve_gru{r}")

            with nc.Block() as block:
                @block.sync
                def _(sp):
                    with sp.Fori(0, NT // 2) as i:
                        for b in range(2):
                            sp.wait_ge(h_new, 2 * i)
                            sp.dma_start(sums[b][:], sums_dram[bass.ds((2 * i + b) * P, P), :]).then_inc(sums_got[b], 16)

                @block.tensor
                def _(te):
                    with te.Fori(0, NT // 2) as i:
                        for b in range(2):
                            k = 2 * i + b
                            te.wait_ge(cur_ready, k + 1)
                            te.wait_ge(T_ready, 2 * k)
                            nc.tensor.transpose(ps_T[0:HA, P:2 * P], hcur[b][:], ident[:])
                            nc.tensor.transpose(ps_T[0:H, 0:P], sums[b][:, 0:H], ident[:]).then_inc(T_turned, 1)
                            te.wait_ge(T_ready, 2 * k + 2)
                            te.wait_ge(h_new, 2 * i)
                            nc.tensor.matmul(ps_gates[b][:, 0:4 * H + G], hT[b][:], w_node[:, r, :], start=True, stop=False)
                            nc.tensor.matmul(ps_gates[b][:, 0:G], sumT[b][:], w_sum[:, r, :], start=False,
                                             stop=True).then_inc(gates_ready, 1)

                @block.scalar
                def _(act):
                    with act.Fori(0, NT // 2) as i:
                        for b in range(2):
                            k = 2 * i + b
                            act.wait_ge(T_turned, k + 1)
                            act.wait_ge(gates_ready, 2 * i)
                            nc.scalar.activation(sumT[b][:], ps_T[0:H, 0:P], ACT.Copy).then_inc(T_ready, 1)
                            nc.scalar.activation(hT[b][:], ps_T[0:HA, P:2 * P], ACT.Copy).then_inc(T_ready, 1)
                            act.wait_ge(gi_ready, k + 1)
                            nc.scalar.activation(rz[b][:], gi[b][:, 0:2 * H], ACT.Sigmoid).then_inc(rz_ready, 1)
                            act.wait_ge(tn_ready, k + 1)
                            nc.scalar.activation(cand[b][:], tn[b][:], ACT.Tanh).then_inc(cand_ready, 1)

                @block.vector
                def _(dve):
                    with dve.Fori(0, NT // 2) as i:
                        for b in range(2):
                            k = 2 * i + b
                            own = lambda n: 5 * k + n
                            dve.wait_ge(sums_got[b], 16 * i + 16)
                            nc.vector.tensor_copy(h[:, bass.ds(k, 1), H:H + 1],
                                                  sums[b][:, H:H + 1].rearrange("p (o f) -> p o f", o=1)).then_inc(dve_gru, 1)
                            dve.wait_ge(dve_gru, own(1))
                            nc.vector.tensor_copy(hcur[b][:].rearrange("p (o f) -> p o f", o=1),
                                                  h[:, bass.ds(k, 1), :]).then_inc(cur_ready, 1)
                            dve.wait_ge(gates_ready, k + 1)
                            nc.vector.tensor_copy(gi[b][:], ps_gates[b][:, 0:G]).then_inc(dve_gru, 1)
                            dve.wait_ge(dve_gru, own(2))
                            nc.vector.scalar_tensor_tensor(out=gi[b][:], in0=ps_gates[b][:, 4 * H:4 * H + G],
                                                           scalar=sums[b][:, H + 1:HA], in1=gi[b][:],
                                                           op0=ALU.mult, op1=ALU.add).then_inc(gi_ready, 1)
                            dve.wait_ge(gi_ready, k + 1)
                            dve.wait_ge(rz_ready, k + 1)
                            nc.vector.tensor_tensor(tn[b][:], rz[b][:, 0:H], ps_gates[b][:, G:4 * H], ALU.mult).then_inc(dve_gru, 1)
                            dve.wait_ge(dve_gru, own(3))
                            nc.vector.tensor_tensor(tn[b][:], tn[b][:], gi[b][:, 2 * H:G], ALU.add).then_inc(tn_ready, 1)
                            dve.wait_ge(cand_ready, k + 1)
                            dve.wait_ge(cur_ready, k + 1)
                            nc.vector.tensor_tensor(tn[b][:], hcur[b][:, 0:H], cand[b][:], ALU.subtract).then_inc(dve_gru, 1)
                            dve.wait_ge(dve_gru, own(4))
                            nc.vector.tensor_tensor(tn[b][:], tn[b][:], rz[b][:, H:2 * H], ALU.mult).then_inc(dve_gru, 1)
                            dve.wait_ge(dve_gru, own(5))
                            nc.vector.tensor_tensor(h[:, bass.ds(k, 1), 0:H], tn[b][:].rearrange("p (o f) -> p o f", o=1),
                                                    cand[b][:].rearrange("p (o f) -> p o f", o=1), ALU.add).then_inc(h_new, 1)

        x_again = sem("x_again")
        added = sem("added")
        result = sem("result")
        with nc.Block() as block:
            @block.sync
            def _(sp):
                with nc.allow_non_contiguous_dma(reason="rows of nodes"):
                    sp.dma_start(wide[:, 0:NT - 1, :], x[0:(NT - 1) * P, :].rearrange("(t p) f -> p t f", p=P)).then_inc(x_again, 16)
                    sp.dma_start(wide[0:TAIL, NT - 1, :], x[(NT - 1) * P:N, :]).then_inc(x_again, 16)
                    sp.wait_ge(added, 1)
                    sp.dma_start(out[0:(NT - 1) * P, :].rearrange("(t p) f -> p t f", p=P), wide[:, 0:NT - 1, :]).then_inc(result, 16)
                    sp.dma_start(out[(NT - 1) * P:N, :], wide[0:TAIL, NT - 1, :]).then_inc(result, 16)
                sp.wait_ge(result, 32)

            @block.vector
            def _(dve):
                dve.wait_ge(x_again, 32)
                nc.vector.tensor_tensor(wide[:], wide[:], h[:, :, 0:H], ALU.add).then_inc(added, 1)


_INS = ["x", "src", "dst", "edge_weight1", "L0_gnn_msg_W", "L0_gnn_msg_b", "L0_gnn_gru_Wih", "L0_gnn_gru_bih",
        "L0_gnn_gru_Whh", "L0_gnn_gru_bhh"]


def kernel(**inputs):
    import numpy as _np
    import concourse.bacc as _bacc
    from concourse import mybir as _mybir
    from concourse.bass_utils import run_bass_kernel_spmd as _run

    nc = _bacc.Bacc("TRN2", target_bir_lowering=False, num_devices=1)
    arrays, args = {}, []
    for name in _INS:
        a = _np.ascontiguousarray(inputs[name])
        arrays[f"in_{name}_dram"] = a
        args.append(nc.dram_tensor(f"in_{name}_dram", a.shape, _mybir.dt.from_np(a.dtype), kind="ExternalInput").ap())
    out = nc.dram_tensor("out_0_dram", inputs["x"].shape, F32, kind="ExternalOutput").ap()
    build(nc, *args, out)
    r = _run(nc, [arrays], core_ids=[0])
    return r.results[0]["out_0_dram"]
```

```python
from contextlib import ExitStack

import concourse.bass as bass
from concourse import mybir

P = 128
F32 = mybir.dt.float32
F16 = mybir.dt.float16
BF16 = mybir.dt.bfloat16
I32 = mybir.dt.int32
ALU = mybir.AluOpType
ACT = mybir.ActivationFunctionType
AX = mybir.AxisListType
EPS = 1e-5
SLOTS = 64
BIG = 2048.0
LO = 2048.0
UJ = 4
NQ = 4
TENSOR_PATH, GENERAL_PATH = 0, 1
PEELED = 4
LAG = 2


class Chain:

    def __init__(self, engine, sem):
        self.engine, self.sem, self.at = engine, sem, 0

    def __call__(self, ins):
        self.at += 1
        ins.then_inc(self.sem, 1)
        self.engine.wait_ge(self.sem, self.at)


def wait(engine, sem, value):
    if not isinstance(value, int) or value > 0:
        engine.wait_ge(sem, value)


def past(i, n):
    return not isinstance(i, int) or i >= n


def in_pairs(engine, n, body):
    for i in range(min(PEELED, n)):
        body(i, i % 2, i // 2)
    if n // 2 > PEELED // 2:
        with engine.Fori(PEELED // 2, n // 2) as i:
            body(2 * i, 0, i)
            body(2 * i + 1, 1, i)
    if n % 2 and n > PEELED:
        body(n - 1, 0, n // 2)


def tiles_per_chunk(tiles, nodes, node_tiles):
    edges = tiles * P
    fits = [k for k in range(1, tiles + 1)
            if tiles % k == 0 and k * P * nodes <= 0.8 * P * edges and k * P <= 0.52 * SLOTS * node_tiles]
    return max(fits)


def split(t, a):
    return t.rearrange("p (a b) -> p a b", a=a)


def along(t, n):
    return t.rearrange("p (a o) -> p a o", o=1).broadcast_to([t.shape[0], t.shape[1], n])


def across(t, n):
    return t.rearrange("p (o b) -> p o b", o=1).broadcast_to([t.shape[0], n, t.shape[1]])


def build(nc, x, src, dst, attr, msg_W, msg_b, Wih, bih, Whh, bhh, out):
    N, H = x.shape
    E = src.shape[0]
    ROUNDS = msg_W.shape[0]
    NT = -(-N // P)
    NP = NT * P
    TAIL = N - (NT - 1) * P
    ET = E // P
    CT = tiles_per_chunk(ET, N, NT)
    C = ET // CT
    GT = max(k for k in range(1, CT + 1) if CT % k == 0 and k * NT <= 512)
    NG = CT // GT
    J = -(-C // 2)
    NU = -(-J // UJ)
    UQ = -(-NU // NQ)
    QC = UQ * UJ * 2
    assert E % P == 0 and H == 64 and NT % 2 == 0 and NU > (NQ - 1) * UQ and UQ >= LAG and N >= P
    HA = H + 2
    G = 3 * H
    SKIP = float(1 << 22)

    def pairs_of(u):
        return range(u * UJ, min(u * UJ + UJ, J))

    SUM_AT, TURN_AT, GATES_AT, SIGMOID_AT, TANH_AT = [min(k, NU - 2) for k in (3, 7, 11, 15, 1)]

    def units_of(q):
        return range(q * UQ, min(q * UQ + UQ, NU))

    with ExitStack() as ctx:
        names_taken = {}

        def unused(name):
            names_taken[name] = names_taken.get(name, 0) + 1
            return f"{name}_{names_taken[name]}" if names_taken[name] > 1 else name

        def sb(name, shape, dt=F32, scope=ctx):
            return scope.enter_context(nc.sbuf_tensor(unused(name), shape, dt))

        def ps(name, shape, dt=F32, scope=ctx):
            return scope.enter_context(nc.psum_tensor(unused(name), shape, dt))

        def sem(name):
            return ctx.enter_context(nc.semaphore(name))

        def dram(name, shape, dt=F32):
            return nc.dram_tensor(name, shape, dt, kind="Internal").ap()

        def gru_buffers(scope):
            return [[sb(f"{name}{b}", shape, scope=scope) for b in range(2)] for name, shape in
                    (("hcur", [P, HA]), ("sumT", [P, P]), ("hT", [HA, P]), ("gi", [P, G]), ("rz", [P, 2 * H]),
                     ("tn", [P, H]), ("cand", [P, H]))]

        h_dram = dram("h_dram", [NP, H])
        sums_dram = dram("sums_dram", [NP, HA])
        parts_dram = dram("parts_dram", [NP, 2 * H], F16)
        lanes_dram = dram("lanes_dram", [NT, NQ * QC * SLOTS], F16)

        h = sb("h", [P, NT, HA])
        ident = sb("ident", [P, P])
        earlier = sb("earlier", [P, P])
        later = sb("later", [P, P])
        lane_no = sb("lane_no", [P, 1])
        lane_no_i = sb("lane_no_i", [P, 1], I32)
        begun = sem("begun")

        def plain(ins):
            return ins.wait_op(begun, 1, "sem-ge")

        ones = sb("ones", [P, P])
        zeros = sb("zeros", [P, HA])
        wmsg = sb("wmsg", [H, ROUNDS, 2 * H + 2])
        wmsg_parts = sb("wmsg_parts", [H, ROUNDS, 2 * H])
        pick = sb("pick", [HA, 2])
        w_sum = sb("w_sum", [P, ROUNDS, G])
        w_node = sb("w_node", [HA, ROUNDS, 4 * H + G])
        iota = sb("iota", [P, P], F16)
        degree = sb("degree", [P, NT])
        src_lane = sb("src_lane", [P, J, NT], F16)
        first = sb("first", [1, C], I32)
        misfit = sb("misfit", [1, 1], I32)

        padded = sem("padded")
        const = sem("const")
        inputs = sem("inputs")
        cleared = sem("cleared")
        var_ready = sem("var_ready")
        std_ready = sem("std_ready")
        turned = sem("turned")
        gate_w = sem("gate_w")
        biases = sem("biases")
        folded = sem("folded")
        fold_used = sem("fold_used")
        parts_ready = sem("parts_ready")
        dve_own = sem("dve_own")
        N_CONST, N_INPUTS, N_BIASES = 9, 16 * (4 + 2 * ROUNDS), 16 * 3 * ROUNDS

        prep_scope = ctx.enter_context(ExitStack())
        wih = sb("wih", [H, 3, ROUNDS, H], scope=prep_scope)
        whh = sb("whh", [H, 3, ROUNDS, H], scope=prep_scope)
        wihT = sb("wihT", [H, ROUNDS, G], scope=prep_scope)
        bias = sb("bias", [HA, ROUNDS, 4 * H], scope=prep_scope)
        wide = sb("wide", [P, NT, H], scope=prep_scope)
        total, mean, var, std, newton, rstd = [sb(n, [P, NT], scope=prep_scope)
                                               for n in ("total", "mean", "var", "std", "newton", "rstd")]
        iota_i = sb("iota_i", [P, P], I32, scope=prep_scope)
        ps_a = ps("ps_a", [P, 512], scope=prep_scope)
        ps_b = ps("ps_b", [P, 512], scope=prep_scope)

        with nc.Block() as block:
            @block.sync
            def _(sp):
                with nc.allow_non_contiguous_dma(reason="small weights"):
                    sp.wait_ge(padded, 1)
                    sp.dma_start(h[:, 0:NT - 1, 0:H],
                                 x[0:(NT - 1) * P, :].rearrange("(t p) f -> p t f", p=P)).then_inc(inputs, 16)
                    sp.dma_start(h[0:TAIL, NT - 1, 0:H], x[(NT - 1) * P:N, :]).then_inc(inputs, 16)
                    sp.dma_start(wmsg[:, :, 0:2 * H + 1], msg_W.rearrange("r m k -> m r k")).then_inc(inputs, 16)
                    sp.dma_start(wmsg[:, :, 2 * H + 1:2 * H + 2],
                                 msg_b.rearrange("r (m o) -> m r o", o=1)).then_inc(inputs, 16)
                    for r in range(ROUNDS):
                        sp.dma_start(wih[:, :, r, :], Wih[r].rearrange("(g m) k -> m g k", g=3)).then_inc(inputs, 16)
                        sp.dma_start(whh[:, :, r, :], Whh[r].rearrange("(g m) k -> m g k", g=3)).then_inc(inputs, 16)
                    sp.wait_ge(cleared, 2)
                    for r in range(ROUNDS):
                        sp.dma_start(w_node[HA - 1:HA, r, 0:G], bih[r:r + 1, :]).then_inc(biases, 16)
                        sp.dma_start(bias[HA - 1:HA, r, 0:2 * H], bhh[r:r + 1, 0:2 * H]).then_inc(biases, 16)
                        sp.dma_start(bias[HA - 1:HA, r, 3 * H:4 * H], bhh[r:r + 1, 2 * H:G]).then_inc(biases, 16)

            @block.gpsimd
            def _(pool):
                nc.gpsimd.memset(h[:, NT - 1, 0:H], 0.0).then_inc(padded, 1)
                nc.gpsimd.iota(lane_no_i[:], pattern=[[0, 1]], base=0, channel_multiplier=1).then_inc(const, 1)
                nc.gpsimd.iota(iota_i[:], pattern=[[1, P]], base=0, channel_multiplier=0).then_inc(const, 1)
                nc.gpsimd.memset(zeros[:], 0.0).then_inc(const, 1)
                nc.gpsimd.memset(ones[:], 1.0).then_inc(const, 1)
                pool.wait_ge(const, 4)
                nc.gpsimd.affine_select(out=ident[:], in_=ones[:], compare_op=ALU.is_equal, fill=0.0, base=0,
                                        pattern=[[-1, P]], channel_multiplier=1).then_inc(const, 1)
                nc.gpsimd.affine_select(out=earlier[:], in_=ones[:], compare_op=ALU.is_gt, fill=0.0, base=0,
                                        pattern=[[-1, P]], channel_multiplier=1).then_inc(const, 1)
                nc.gpsimd.affine_select(out=later[:], in_=ones[:], compare_op=ALU.is_gt, fill=0.0, base=0,
                                        pattern=[[1, P]], channel_multiplier=-1).then_inc(const, 1)
                nc.gpsimd.affine_select(out=pick[:, 0:1], in_=ones[0:HA, 0:1], compare_op=ALU.is_equal, fill=0.0,
                                        base=-H, pattern=[[0, 1]], channel_multiplier=1).then_inc(const, 1)
                nc.gpsimd.affine_select(out=pick[:, 1:2], in_=ones[0:HA, 0:1], compare_op=ALU.not_equal, fill=0.0,
                                        base=-H, pattern=[[0, 1]], channel_multiplier=1).then_inc(const, 1)

            @block.tensor
            def _(te):
                te.wait_ge(inputs, N_INPUTS)
                te.wait_ge(const, N_CONST)
                for r in range(ROUNDS):
                    if r:
                        te.wait_ge(gate_w, 3 * r)
                    for g in range(3):
                        nc.tensor.transpose(ps_a[0:H, g * H:(g + 1) * H], wih[:, g, r, :], ident[0:H, 0:H])
                        last = nc.tensor.transpose(ps_b[0:H, g * H:(g + 1) * H], whh[:, g, r, :], ident[0:H, 0:H])
                    last.then_inc(turned, 1)
                te.wait_ge(gate_w, 3 * ROUNDS)
                te.wait_ge(parts_ready, 2)
                for r in range(ROUNDS):
                    if r:
                        te.wait_ge(fold_used, 3 * r)
                    nc.tensor.matmul(ps_a[:, 0:G], wmsg_parts[:, r, :], wihT[:, r, :], start=True, stop=True)
                    nc.tensor.matmul(ps_b[0:HA, 0:G], wmsg[:, r, H:2 * H + 2], wihT[:, r, :], start=True,
                                     stop=True).then_inc(folded, 1)

            @block.scalar
            def _(act):
                act.wait_ge(var_ready, 1)
                nc.scalar.activation(std[:], var[:], ACT.Sqrt).then_inc(std_ready, 1)
                act.wait_ge(cleared, 2)
                for r in range(ROUNDS):
                    act.wait_ge(turned, r + 1)
                    nc.scalar.activation(wihT[:, r, :], ps_a[0:H, 0:G], ACT.Copy).then_inc(gate_w, 1)
                    nc.scalar.activation(w_node[0:H, r, 0:2 * H], ps_b[0:H, 0:2 * H], ACT.Copy).then_inc(gate_w, 1)
                    nc.scalar.activation(w_node[0:H, r, 3 * H:4 * H], ps_b[0:H, 2 * H:G], ACT.Copy).then_inc(gate_w, 1)

            @block.vector
            def _(dve):
                step = Chain(dve, dve_own)
                rows = h[:, :, 0:H]

                def per_row(t):
                    return t[:].rearrange("p (t o) -> p t o", o=1).broadcast_to([P, NT, H])

                nc.vector.memset(w_node[:], 0.0).then_inc(cleared, 1)
                nc.vector.memset(bias[:], 0.0).then_inc(cleared, 1)
                step(nc.vector.memset(h[:, :, H:H + 1], 0.0))
                step(nc.vector.memset(h[:, :, H + 1:HA], 1.0))
                dve.wait_ge(inputs, N_INPUTS)
                dve.wait_ge(const, N_CONST)
                nc.vector.tensor_copy(iota[:], iota_i[:])
                nc.vector.tensor_copy(lane_no[:], lane_no_i[:]).then_inc(begun, 1)
                nc.vector.tensor_copy(wmsg_parts[:, :, 0:H], wmsg[:, :, 0:H]).then_inc(parts_ready, 1)
                nc.vector.tensor_scalar(wmsg_parts[:, :, H:2 * H], wmsg[:, :, 0:H], 1.0 / LO, None,
                                        ALU.mult).then_inc(parts_ready, 1)
                step(nc.vector.tensor_reduce(total[:], rows, AX.X, ALU.add))
                step(nc.vector.tensor_scalar(mean[:], total[:], 1.0 / H, None, ALU.mult))
                step(nc.vector.tensor_tensor(rows, rows, per_row(mean), ALU.subtract))
                step(nc.vector.tensor_tensor(wide[:], rows, rows, ALU.mult))
                step(nc.vector.tensor_reduce(total[:], wide[:], AX.X, ALU.add))
                nc.vector.tensor_scalar(var[:], total[:], 1.0 / H, EPS, ALU.mult, ALU.add).then_inc(var_ready, 1)
                dve.wait_ge(std_ready, 1)
                step(nc.vector.reciprocal(newton[:], std[:]))
                step(nc.vector.tensor_tensor(newton[:], newton[:], var[:], ALU.mult))
                step(nc.vector.tensor_tensor(newton[:], newton[:], std[:], ALU.add))
                step(nc.vector.tensor_scalar(newton[:], newton[:], 0.5, None, ALU.mult))
                step(nc.vector.reciprocal(rstd[:], newton[:]))
                step(nc.vector.tensor_tensor(rows, rows, per_row(rstd), ALU.mult))
                step(nc.vector.tensor_scalar(rows, rows, 0.0, None, ALU.max))
                dve.wait_ge(gate_w, 3 * ROUNDS)
                dve.wait_ge(biases, N_BIASES)
                for r in range(ROUNDS):
                    step(nc.vector.tensor_tensor(w_node[:, r, 0:4 * H], w_node[:, r, 0:4 * H], bias[:, r, :], ALU.add))
                    dve.wait_ge(folded, r + 1)
                    nc.vector.tensor_copy(w_sum[:, r, :], ps_a[:, 0:G]).then_inc(fold_used, 1)
                    nc.vector.scalar_tensor_tensor(out=w_node[:, r, 0:G], in0=ps_b[0:HA, 0:G], scalar=pick[:, 0:1],
                                                   in1=w_node[:, r, 0:G], op0=ALU.mult, op1=ALU.add).then_inc(fold_used, 1)
                    nc.vector.tensor_scalar(w_node[:, r, 4 * H:4 * H + G], ps_b[0:HA, 0:G], pick[:, 1:2], None,
                                            ALU.mult).then_inc(fold_used, 1)

        prep_scope.close()

        attr_slot = sb("attr_slot", [P, J, NT])
        slot_scope = ctx.enter_context(ExitStack())
        at_slot = sb("at_slot", [P, J, NT], scope=slot_scope)
        loop_scope = ctx.enter_context(ExitStack())
        attr_e = sb("attr_e", [P, C, CT], scope=loop_scope)
        code = sb("code", [P, C, CT], scope=loop_scope)
        tile_e = sb("tile_e", [P, C, CT], F16, scope=loop_scope)
        twins = sb("twins", [P, C, CT], F16, scope=loop_scope)
        worst = sb("worst", [P, CT], scope=loop_scope)
        stray = sb("stray", [P, 2], scope=loop_scope)
        edge_scope = ctx.enter_context(ExitStack())
        src_i = sb("src_i", [P, C, CT], I32, scope=edge_scope)
        dst_i = sb("dst_i", [P, C, CT], I32, scope=edge_scope)
        part_i = sb("part_i", [P, C, CT], I32, scope=edge_scope)
        lane_f = sb("lane_f", [P, C, CT], scope=edge_scope)
        alike = sb("alike", [P, C, CT], F16, scope=edge_scope)
        firstf = sb("firstf", [1, C], scope=edge_scope)
        first_all = sb("first_all", [P, C], scope=edge_scope)
        ps_first = ps("ps_first", [P, 512], scope=edge_scope)

        edges_in = sem("edges_in")
        firstf_ready = sem("firstf_ready")
        first_ps = sem("first_ps")
        dve_edges = sem("dve_edges")
        with nc.Block() as block:
            @block.sync
            def _(sp):
                with nc.allow_non_contiguous_dma(reason="a lane's edges of every chunk"):
                    sp.dma_start(dst_i[:], dst.rearrange("(c p t) -> p c t", p=P, t=CT)).then_inc(edges_in, 16)
                    sp.dma_start(src_i[:], src.rearrange("(c p t) -> p c t", p=P, t=CT)).then_inc(edges_in, 16)
                    sp.dma_start(attr_e[:], attr.rearrange("(c p t) o -> p c (t o)", p=P, t=CT)).then_inc(edges_in, 16)

            @block.tensor
            def _(te):
                te.wait_ge(firstf_ready, 1)
                nc.tensor.matmul(ps_first[:, 0:C], ones[0:1, :], firstf[:], start=True, stop=True).then_inc(first_ps, 1)

            @block.vector
            def _(dve):
                step = Chain(dve, dve_edges)
                dve.wait_ge(edges_in, 48)
                step(nc.vector.tensor_copy(firstf[:], dst_i[0:1, :, 0]))
                step(nc.vector.tensor_scalar(firstf[:], firstf[:], float(NP - P), 0.0, ALU.min, ALU.max))
                nc.vector.tensor_copy(first[:], firstf[:]).then_inc(firstf_ready, 1)
                dve.wait_ge(first_ps, 1)
                step(nc.vector.tensor_copy(first_all[:], ps_first[:, 0:C]))
                step(nc.vector.tensor_copy(lane_f[:], dst_i[:]))
                step(nc.vector.tensor_tensor(lane_f[:], lane_f[:], along(first_all[:], CT), ALU.subtract))
                step(nc.vector.tensor_reduce(stray[:, 0:1], lane_f[:], AX.XY, ALU.max))
                step(nc.vector.tensor_reduce(stray[:, 1:2], lane_f[:], AX.XY, ALU.min))
                step(nc.vector.tensor_scalar(part_i[:], src_i[:], P - 1, None, ALU.bitwise_and))
                step(nc.vector.tensor_copy(code[:], part_i[:]))
                step(nc.vector.tensor_scalar(code[:], code[:], float(P), 1.0, ALU.mult, ALU.add))
                step(nc.vector.tensor_tensor(code[:], code[:], lane_f[:], ALU.add))
                step(nc.vector.tensor_scalar(part_i[:], src_i[:], 7, None, ALU.arith_shift_right))
                step(nc.vector.tensor_copy(tile_e[:], part_i[:]))
                step(nc.vector.memset(twins[:], 0.0))
                for d in range(1, CT):
                    step(nc.vector.tensor_tensor(alike[:, :, d:], tile_e[:, :, d:], tile_e[:, :, 0:CT - d], ALU.is_equal))
                    step(nc.vector.tensor_tensor(twins[:, :, d:], twins[:, :, d:], alike[:, :, d:], ALU.add))
                step(nc.vector.memset(worst[:], 0.0))
                step(nc.vector.memset(at_slot[:], 0.0))
                step(nc.vector.memset(attr_slot[:], 0.0))
        edge_scope.close()

        lift = sb("lift", [P, P], F16, scope=loop_scope)
        unit16 = sb("unit16", [P, P], F16, scope=loop_scope)
        before16 = sb("before16", [P, P], F16, scope=loop_scope)
        pair = range(2)
        onehot = [sb(f"onehot{b}", [P, CT, NT], F16, scope=loop_scope) for b in pair]
        onehot32 = [sb(f"onehot32{b}", [P, CT, NT], scope=loop_scope) for b in pair]
        lanes_before = [sb(f"lanes_before{b}", [P, NT], F16, scope=loop_scope) for b in pair]
        top = [sb(f"top{b}", [P, CT], scope=loop_scope) for b in pair]
        rank = [sb(f"rank{b}", [P, CT], scope=loop_scope) for b in pair]
        slot1 = [sb(f"slot1{b}", [P, CT, SLOTS], scope=loop_scope) for b in pair]
        placed_vals = [sb(f"placed_vals{b}", [P, CT, 2, SLOTS], scope=loop_scope) for b in pair]
        ps_before_bank = [ps(f"ps_before{b}", [P, 512], scope=loop_scope) for b in pair]
        ps_count_bank = [ps(f"ps_count{b}", [P, 512], scope=loop_scope) for b in pair]
        ps_slots_bank = [ps(f"ps_slots{b}", [P, 512], scope=loop_scope) for b in pair]

        ps_check = ps("ps_check", [P, 512], scope=loop_scope)
        ps_before = [t[:, 0:NT] for t in ps_before_bank]
        ps_count = [t[:, 0:GT * NT].rearrange("p (a b) -> p a b", a=GT) for t in ps_count_bank]
        ps_slots = [t[:, 0:NT] for t in ps_slots_bank]

        mats = sem("mats")
        onehot_ready = sem("onehot_ready")
        onehot32_ready = sem("onehot32_ready")
        before_ps = sem("before_ps")
        before_ready = sem("before_ready")
        count_ps = sem("count_ps")
        top_ready = sem("top_ready")
        rank_ready = sem("rank_ready")
        slot_ready = sem("slot_ready")
        code_ready = sem("code_ready")
        attr_ready = sem("attr_ready")
        slots_ps = sem("slots_ps")
        slots_kept = sem("slots_kept")
        worst_ready = sem("worst_ready")

        with nc.Block() as block:
            @block.tensor
            def _(te):
                te.wait_ge(mats, 3)

                def place(c, b):
                    te.wait_ge(code_ready, c + 1)
                    te.wait_ge(attr_ready, c + 1)
                    te.wait_ge(onehot32_ready, c + 1)
                    wait(te, slots_kept, 2 * (c - 1))
                    for t in range(CT):
                        last = nc.tensor.matmul(ps_slots[b][:], placed_vals[b][:, t, :, :].rearrange("p v s -> p (v s)"),
                                                onehot32[b][:, t, :], start=(t == 0), stop=(t == CT - 1))
                    last.then_inc(slots_ps, 1)

                def body(c, b, half):
                    te.wait_ge(onehot_ready, c + 1)
                    wait(te, before_ready, c - 1)
                    for t in range(CT):
                        last = nc.tensor.matmul(ps_before[b], before16[:], onehot[b][:, t, :],
                                                start=(t == 0), stop=(t == CT - 1))
                    last.then_inc(before_ps, 1)
                    te.wait_ge(before_ready, c + 1)
                    for g in range(NG):
                        wait(te, top_ready, c * NG + g - 1)
                        n = (c * NG + g) % 2 if isinstance(c, int) else (b * NG + g) % 2
                        nc.tensor.matmul(ps_count[n], unit16[:], across(lanes_before[b][:], GT), start=True, stop=False)
                        nc.tensor.matmul(ps_count[n], lift[:], onehot[b][:, g * GT:(g + 1) * GT, :], start=False,
                                         stop=True).then_inc(count_ps, 1)
                    if past(c, 1):
                        place(c - 1, 1 - b)

                in_pairs(te, C, body)
                place(C - 1, (C - 1) % 2)

            @block.scalar
            def _(act):
                def keep(c, b, half):
                    act.wait_ge(slots_ps, c + 1)
                    lanes = slice(b * SLOTS, b * SLOTS + SLOTS)
                    plain(nc.scalar.activation(at_slot[lanes, bass.ds(half, 1), :].rearrange("p o s -> p (o s)"),
                                               ps_slots[b][0:SLOTS, :], ACT.Copy)).then_inc(slots_kept, 1)
                    plain(nc.scalar.activation(attr_slot[lanes, bass.ds(half, 1), :].rearrange("p o s -> p (o s)"),
                                               ps_slots[b][SLOTS:2 * SLOTS, :], ACT.Copy)).then_inc(slots_kept, 1)

                def body(c, b, half):
                    act.wait_ge(before_ps, c + 1)
                    wait(act, count_ps, (c - 1) * NG)
                    nc.scalar.activation(lanes_before[b][:], ps_before[b], ACT.Copy).then_inc(before_ready, 1)
                    wait(act, slots_ps, c - 1)
                    nc.scalar.activation(onehot32[b][:], onehot[b][:], ACT.Copy).then_inc(onehot32_ready, 1)
                    if past(c, 1):
                        keep(c - 1, 1 - b, half - 1 + b)

                in_pairs(act, C, body)
                keep(C - 1, (C - 1) % 2, (C - 1) // 2)

            @block.gpsimd
            def _(pool):
                def body(c, b, half):
                    pool.wait_ge(slot_ready, c + 1)
                    wait(pool, slots_ps, c - 1)
                    plain(nc.gpsimd.tensor_tensor(placed_vals[b][:, :, 1, :], slot1[b][:],
                                                  along(attr_e[:, bass.ds(c, 1), :].rearrange("p o t -> p (o t)"), SLOTS),
                                                  ALU.mult)).then_inc(attr_ready, 1)

                in_pairs(pool, C, body)

            @block.vector
            def _(dve):
                nc.vector.tensor_scalar(lift[:], ident[:], BIG, None, ALU.mult).then_inc(mats, 1)
                nc.vector.tensor_copy(unit16[:], ident[:]).then_inc(mats, 1)
                nc.vector.tensor_copy(before16[:], later[:]).then_inc(mats, 1)

                def hot(c, b):
                    wait(dve, count_ps, (c - 1) * NG)
                    wait(dve, onehot32_ready, c - 1)
                    nc.vector.tensor_tensor(onehot[b][:], across(iota[:, 0:NT], CT),
                                            along(tile_e[:, bass.ds(c, 1), :].rearrange("p o t -> p (o t)"), NT),
                                            ALU.is_equal).then_inc(onehot_ready, 1)

                def place(c, b):
                    wait(dve, attr_ready, c - 1)
                    nc.vector.tensor_tensor(slot1[b][:], across(iota[:, 0:SLOTS], CT), along(rank[b][:], SLOTS),
                                            ALU.is_equal).then_inc(slot_ready, 1)
                    dve.wait_ge(slot_ready, c + 1)
                    wait(dve, slots_ps, c - 1)
                    nc.vector.tensor_tensor(placed_vals[b][:, :, 0, :], slot1[b][:],
                                            along(code[:, bass.ds(c, 1), :].rearrange("p o t -> p (o t)"), SLOTS),
                                            ALU.mult).then_inc(code_ready, 1)

                def body(c, b, half):
                    hot(c, b)
                    if past(c, 1):
                        place(c - 1, 1 - b)
                    for g in range(NG):
                        dve.wait_ge(count_ps, c * NG + g + 1)
                        n = (c * NG + g) % 2 if isinstance(c, int) else (b * NG + g) % 2
                        nc.vector.tensor_reduce(top[b][:, g * GT:(g + 1) * GT], ps_count[n], AX.X,
                                                ALU.max).then_inc(top_ready, 1)
                    dve.wait_ge(top_ready, (c + 1) * NG)
                    wait(dve, slot_ready, c - 1)
                    nc.vector.scalar_tensor_tensor(out=rank[b][:], in0=top[b][:], scalar=-BIG,
                                                   in1=twins[:, bass.ds(c, 1), :].rearrange("p o t -> p (o t)"),
                                                   op0=ALU.add, op1=ALU.add).then_inc(rank_ready, 1)
                    dve.wait_ge(rank_ready, c + 1)
                    wait(dve, worst_ready, c)
                    nc.vector.tensor_tensor(worst[:], worst[:], rank[b][:], ALU.max).then_inc(worst_ready, 1)

                in_pairs(dve, C, body)
                place(C - 1, (C - 1) % 2)
                dve.wait_ge(worst_ready, C)

        check_ready = sem("check_ready")
        check_ps = sem("check_ps")
        limit_ready = sem("limit_ready")
        limits = sb("limits", [3, P], scope=loop_scope)
        check = sb("check", [P, 3], scope=loop_scope)
        over = sb("over", [3, 4], scope=loop_scope)
        dve_check = sem("dve_check")
        over_ready = sem("over_ready")
        over_ps = sem("over_ps")
        with nc.Block() as block:
            @block.tensor
            def _(te):
                te.wait_ge(check_ready, 1)
                nc.tensor.transpose(ps_check[0:3, 0:P], check[:], ident[:]).then_inc(check_ps, 1)
                te.wait_ge(over_ready, 1)
                nc.tensor.matmul(ps_check[0:1, P:P + 1], over[:, 3:4], ones[0:3, 0:1], start=True, stop=True).then_inc(over_ps, 1)

            @block.vector
            def _(dve):
                step = Chain(dve, dve_check)
                step(nc.vector.tensor_reduce(check[:, 0:1], worst[:], AX.X, ALU.max))
                step(nc.vector.tensor_scalar(check[:, 0:1], check[:, 0:1], float(SLOTS - 1), None, ALU.subtract))
                step(nc.vector.tensor_scalar(check[:, 1:2], stray[:, 0:1], float(P - 1), None, ALU.subtract))
                nc.vector.tensor_scalar(check[:, 2:3], stray[:, 1:2], -1.0, None, ALU.mult).then_inc(check_ready, 1)
                dve.wait_ge(check_ps, 1)
                step(nc.vector.tensor_reduce(over[:, 2:3], ps_check[0:3, 0:P], AX.X, ALU.max))
                nc.vector.tensor_scalar(over[:, 3:4], over[:, 2:3], 0.0, None, ALU.is_gt).then_inc(over_ready, 1)
                dve.wait_ge(over_ps, 1)
                step(nc.vector.tensor_scalar(misfit[:], ps_check[0:1, P:P + 1], 1.0, None, ALU.min))
        loop_scope.close()

        slot_i = sb("slot_i", [P, J, NT], I32, scope=slot_scope)
        dst_lane = sb("dst_lane", [P, J, NT], scope=slot_scope)
        lanes_T = [sb(f"lanes_T{b}", [NT, UJ * P], F16, scope=slot_scope) for b in pair]
        ps_lanes = [ps(f"ps_lanes{b}", [P, UJ * P], scope=slot_scope) for b in pair]
        unpacked = sem("unpacked")
        lanes_ps = sem("lanes_ps")
        lanes_ready = sem("lanes_ready")
        lanes_out = [sem(f"lanes_out{b}") for b in pair]
        dve_unpack = sem("dve_unpack")
        lane_i = at_slot[:].bitcast(I32)
        with nc.Block() as block:
            @block.vector
            def _(dve):
                step = Chain(dve, dve_unpack)
                step(nc.vector.tensor_scalar(at_slot[:], at_slot[:], -1.0, None, ALU.add))
                step(nc.vector.tensor_copy(slot_i[:], at_slot[:]))
                step(nc.vector.tensor_scalar(lane_i, slot_i[:], P - 1, None, ALU.bitwise_and))
                nc.vector.tensor_copy(dst_lane[:], lane_i).then_inc(unpacked, 1)
                step(nc.vector.tensor_scalar(slot_i[:], slot_i[:], 7, None, ALU.arith_shift_right))
                step(nc.vector.tensor_copy(src_lane[:], slot_i[:]))

            @block.tensor
            def _(te):
                te.wait_ge(unpacked, 1)
                for u in range(NU):
                    wait(te, lanes_ready, u - 1)
                    for k, j in enumerate(pairs_of(u)):
                        last = nc.tensor.transpose(ps_lanes[u % 2][0:NT, k * P:(k + 1) * P], dst_lane[:, j, :], ident[:])
                    last.then_inc(lanes_ps, 1)

            @block.scalar
            def _(act):
                for u in range(NU):
                    act.wait_ge(lanes_ps, u + 1)
                    wait(act, lanes_out[u % 2], 16 * (u // 2))
                    n = len(pairs_of(u)) * P
                    nc.scalar.activation(lanes_T[u % 2][:, 0:n], ps_lanes[u % 2][0:NT, 0:n], ACT.Copy).then_inc(lanes_ready, 1)

            @block.sync
            def _(sp):
                for u in range(NU):
                    n = len(pairs_of(u)) * P
                    sp.wait_ge(lanes_ready, u + 1)
                    sp.dma_start(lanes_dram[:, u * UJ * P:u * UJ * P + n], lanes_T[u % 2][:, 0:n]).then_inc(lanes_out[u % 2], 16)
                for b in pair:
                    wait(sp, lanes_out[b], 16 * ((NU + 1 - b) // 2))
        slot_scope.close()

        def only(bind, path):
            def bound(program):
                @bind
                def _(engine):
                    taken = engine.value_load(misfit[0:1, 0:1], min_val=0, max_val=1)
                    with engine.If(taken < 1 if path == TENSOR_PATH else taken > 0):
                        program(engine)
            return bound

        def windows_round(r, scope, rows_of):
            parts_scope = scope.enter_context(ExitStack())
            parts = sb("parts", [P, NT, 2 * H], F16, scope=parts_scope)
            rest = sb("rest", [P, NT, H], scope=parts_scope)
            parts_made = sem(f"parts_made{r}")
            parts_out = sem(f"parts_out{r}")
            windows_in = sem(f"windows_in{r}")
            dve_parts = sem(f"dve_parts{r}")
            with nc.Block() as block:
                @only(block.vector, TENSOR_PATH)
                def _(dve):
                    step = Chain(dve, dve_parts)
                    step(nc.vector.tensor_copy(parts[:, :, 0:H], h[:, :, 0:H]))
                    step(nc.vector.tensor_tensor(rest[:], h[:, :, 0:H], parts[:, :, 0:H], ALU.subtract))
                    nc.vector.tensor_scalar(parts[:, :, H:2 * H], rest[:], LO, None, ALU.mult).then_inc(parts_made, 1)

                @only(block.sync, TENSOR_PATH)
                def _(sp):
                    sp.wait_ge(parts_made, 1)
                    with nc.allow_non_contiguous_dma(reason="rows of nodes"):
                        sp.dma_start(parts_dram.rearrange("(t p) f -> p t f", p=P), parts[:]).then_inc(parts_out, 16)
                    sp.wait_ge(parts_out, 16)
                    with sp.Fori(0, C) as c:
                        at = sp.value_load(first[0:1, bass.ds(c, 1)], min_val=0, max_val=NP - P)
                        sp.dma_start(rows_of[:, bass.ds(c, 1), :].rearrange("p o f -> p (o f)"),
                                     parts_dram[bass.ds(at, P), :]).then_inc(windows_in, 16)
                    sp.wait_ge(windows_in, 16 * C)
            parts_scope.close()

        def sums_round(r, scope):
            rows_of = sb("rows_of", [P, C, 2 * H], F16, scope=scope)
            windows_round(r, scope, rows_of)
            hcur, sumT, hT, gi, rz, tn, cand = gru_buffers(scope)
            lanes = [sb(f"lanes{q}", [P, QC * SLOTS], F16, scope=scope) for q in range(NQ)]
            dst1 = [sb(f"dst1{b}", [P, QC * SLOTS], F16, scope=scope) for b in range(2)]
            src1 = [sb(f"src1{b}", [P, QC // 2, P], F16, scope=scope) for b in range(2)]
            rows = [sb(f"rows{b}", [P, UJ, 2 * H], F16, scope=scope) for b in range(4)]
            attr_left = [sb(f"attr_left{b}", [P, J], scope=scope) for b in range(2)]
            attr_parts = [sb(f"attr_parts{b}", [P, J, 4], BF16, scope=scope) for b in range(2)]
            ps_rows = [ps(f"ps_rows{b}", [P, 512], scope=scope) for b in range(4)]
            nothing = sb("nothing", [P, P], F16, scope=scope)
            sums4 = [sb(f"sums4{b}", [P, 4], scope=scope) for b in range(2)]
            ps_sum = [ps(f"ps_sum{b}", [P, 512], scope=scope) for b in range(2)]
            ps_T = ps("ps_T2", [P, 512], scope=scope)
            ps_gates = ps("ps_gates", [P, 512], scope=scope)

            names = ("rows_zero", "dst1_ready", "src1_ready", "gathered", "rows_ready", "scattered", "parts_ready2",
                     "sum_ready", "sums4_ready", "attr_sum", "cur_ready", "turned2", "hT_ready", "gates_ready2", "gi_half", "gi_ready2",
                     "rz_ready2", "tn_half", "tn_ready2", "cand_ready2", "mixed", "h_new2", "pool_own")
            (rows_zero, dst1_ready, src1_ready, gathered, rows_ready, scattered, parts_ready,
             sum_ready, sums4_ready, attr_sum, cur_ready, turned, hT_ready, gates_ready, gi_half, gi_ready,
             rz_ready, tn_half, tn_ready, cand_ready, mixed, h_new, pool_own) = [sem(f"{n}_{r}") for n in names]
            lanes_in = [sem(f"lanes_in{r}_{q}") for q in range(NQ)]

            def done_with(s, q):
                return s * NU + units_of(q - 2)[-1] + 1 if q >= 2 else (s - 1) * NU + units_of(q - 2 + NQ)[-1] + 1

            with nc.Block() as block:
                @only(block.sync, TENSOR_PATH)
                def _(sp):
                    def body(s, b, half):
                        for q in range(NQ):
                            wait(sp, dst1_ready, (s - 1) * NQ + q + 1)
                            n = min((q + 1) * QC, 2 * J) - q * QC
                            sp.dma_start(lanes[q][:, 0:n * SLOTS],
                                         lanes_dram[bass.ds(s, 1), q * QC * SLOTS:(q * QC + n) * SLOTS]
                                         .broadcast_to([P, n * SLOTS])).then_inc(lanes_in[q], 16)

                    in_pairs(sp, NT, body)

                @only(block.gpsimd, TENSOR_PATH)
                def _(pool):
                    if r:
                        return

                    def body(s, b, half):
                        own = lambda n: pool.wait_ge(pool_own, 5 * s + n)
                        wait(pool, scattered, (s - 1) * NU)
                        part = lambda k: attr_parts[b][:, :, k]
                        plain(nc.gpsimd.tensor_copy(attr_left[b][:], attr_slot[:, :, bass.ds(s, 1)]
                                                    .rearrange("p j o -> p (j o)"))).then_inc(pool_own, 1)
                        nc.gpsimd.memset(part(3), 1.0).then_inc(parts_ready, 1)
                        own(1)
                        plain(nc.gpsimd.tensor_copy(part(0), attr_left[b][:])).then_inc(pool_own, 1)
                        own(2)
                        nc.gpsimd.tensor_tensor(attr_left[b][:], attr_left[b][:], part(0), ALU.subtract).then_inc(pool_own, 1)
                        own(3)
                        plain(nc.gpsimd.tensor_copy(part(1), attr_left[b][:])).then_inc(pool_own, 1)
                        own(4)
                        nc.gpsimd.tensor_tensor(attr_left[b][:], attr_left[b][:], part(1), ALU.subtract).then_inc(pool_own, 1)
                        own(5)
                        plain(nc.gpsimd.tensor_copy(part(2), attr_left[b][:])).then_inc(parts_ready, 1)

                    in_pairs(pool, NT, body)

                @only(block.tensor, TENSOR_PATH)
                def _(te):
                    def gather(s, u):
                        q = u // UQ
                        if u % UQ == 0:
                            te.wait_ge(dst1_ready, s * NQ + q + 1)
                        wait(te, rows_ready, s * NU + u - 3)
                        for k, j in enumerate(pairs_of(u)):
                            for half in range(2):
                                c = 2 * j + half
                                if c < C:
                                    last = nc.tensor.matmul(
                                        ps_rows[u % 4][half * SLOTS:(half + 1) * SLOTS, k * 2 * H:(k + 1) * 2 * H],
                                        dst1[q % 2][:, (c - q * QC) * SLOTS:(c - q * QC + 1) * SLOTS], rows_of[:, c, :],
                                        start=True, stop=True)
                        last.then_inc(gathered, 1)

                    def scatter(s, u, b):
                        q = u // UQ
                        te.wait_ge(rows_ready, s * NU + u + 1)
                        if u % UQ == 0:
                            te.wait_ge(src1_ready, s * NQ + q + 1)
                        if u == 0:
                            wait(te, sum_ready, s - 1)
                            if r == 0:
                                wait(te, sums4_ready, s - 1)
                                te.wait_ge(parts_ready, 2 * s + 2)
                                nc.tensor.matmul(ps_sum[b][:, 0:P + 4], nothing[:],
                                                 src1[0].rearrange("p j l -> p (j l)")[:, 0:P + 4], start=True, stop=False)
                        for k, j in enumerate(pairs_of(u)):
                            hot = src1[q % 2][:, j - q * QC // 2, :]
                            if r == 0:
                                nc.tensor.matmul(ps_sum[b][:, P:P + 4], hot, attr_parts[b][:, j, :],
                                                 start=False, stop=False)
                            last = nc.tensor.matmul(ps_sum[b][:, 0:P], rows[u % 4][:, k, :], hot,
                                                    start=(j == 0 and r > 0), stop=(j == J - 1))
                        last.then_inc(scattered, 1)

                    def turn(k, b):
                        te.wait_ge(cur_ready, k + 1)
                        wait(te, hT_ready, k)
                        nc.tensor.transpose(ps_T[0:HA, 0:P], hcur[b][:], ident[:]).then_inc(turned, 1)

                    def gates(k, b):
                        te.wait_ge(hT_ready, k + 1)
                        te.wait_ge(sum_ready, k + 1)
                        wait(te, tn_ready, k)
                        nc.tensor.matmul(ps_gates[:, 0:4 * H + G], hT[b][:], w_node[:, r, :], start=True, stop=False)
                        nc.tensor.matmul(ps_gates[:, 0:G], sumT[b][:], w_sum[:, r, :], start=False,
                                         stop=True).then_inc(gates_ready, 1)

                    te.wait_ge(rows_zero, 1)

                    def body(s, b, half):
                        later_tile = past(s, 1)
                        for u in range(NU):
                            gather(s, u)
                            if u >= LAG:
                                scatter(s, u - LAG, b)
                            elif later_tile:
                                scatter(s - 1, NU - LAG + u, 1 - b)
                            if later_tile and u == TURN_AT:
                                turn(s - 1, 1 - b)
                            if later_tile and u == GATES_AT:
                                gates(s - 1, 1 - b)

                    in_pairs(te, NT, body)
                    for u in range(NU - LAG, NU):
                        scatter(NT - 1, u, (NT - 1) % 2)
                    turn(NT - 1, (NT - 1) % 2)
                    gates(NT - 1, (NT - 1) % 2)

                @only(block.scalar, TENSOR_PATH)
                def _(act):
                    def take(s, u):
                        act.wait_ge(gathered, s * NU + u + 1)
                        wait(act, scattered, s * NU + u - 3)
                        n = len(pairs_of(u))
                        cut = lambda t: t.rearrange("p (j f) -> p j f", j=UJ)
                        if u == NU - 1 and C % 2:
                            if n > 1:
                                nc.scalar.activation(rows[u % 4][:, 0:n - 1, :], cut(ps_rows[u % 4][:])[:, 0:n - 1, :], ACT.Copy)
                            nc.scalar.activation(rows[u % 4][0:SLOTS, n - 1, :], cut(ps_rows[u % 4][:])[0:SLOTS, n - 1, :],
                                                 ACT.Copy).then_inc(rows_ready, 1)
                        else:
                            nc.scalar.activation(rows[u % 4][:, 0:n, :], cut(ps_rows[u % 4][:])[:, 0:n, :],
                                                 ACT.Copy).then_inc(rows_ready, 1)

                    def take_sum(k, b):
                        act.wait_ge(scattered, (k + 1) * NU)
                        wait(act, gates_ready, k - 1)
                        nc.scalar.activation(sumT[b][:], ps_sum[b][:, 0:P], ACT.Copy).then_inc(sum_ready, 1)
                        if r == 0:
                            wait(act, attr_sum, 2 * (k - 1))
                            nc.scalar.activation(sums4[b][:], ps_sum[b][:, P:P + 4], ACT.Copy).then_inc(sums4_ready, 1)

                    def take_hT(k, b):
                        act.wait_ge(turned, k + 1)
                        nc.scalar.activation(hT[b][:], ps_T[0:HA, 0:P], ACT.Copy).then_inc(hT_ready, 1)

                    def sigmoids(k, b):
                        act.wait_ge(gi_ready, k + 1)
                        nc.scalar.activation(rz[b][:], gi[b][:, 0:2 * H], ACT.Sigmoid).then_inc(rz_ready, 1)

                    def tanhs(k, b):
                        act.wait_ge(tn_ready, k + 1)
                        nc.scalar.activation(cand[b][:], tn[b][:], ACT.Tanh).then_inc(cand_ready, 1)

                    act.wait_ge(rows_zero, 1)

                    def body(s, b, half):
                        one_back = past(s, 1)
                        for u in range(NU):
                            take(s, u)
                            if one_back and u == SUM_AT:
                                take_sum(s - 1, 1 - b)
                            if one_back and u == TURN_AT + 1:
                                take_hT(s - 1, 1 - b)
                            if one_back and u == SIGMOID_AT:
                                sigmoids(s - 1, 1 - b)
                            if past(s, 2) and u == TANH_AT:
                                tanhs(s - 2, b)

                    in_pairs(act, NT, body)
                    b = (NT - 1) % 2
                    tanhs(NT - 2, 1 - b)
                    take_sum(NT - 1, b)
                    take_hT(NT - 1, b)
                    sigmoids(NT - 1, b)
                    tanhs(NT - 1, b)

                @only(block.vector, TENSOR_PATH)
                def _(dve):
                    def one_hots(s, q):
                        n = min((q + 1) * QC, 2 * J) - q * QC
                        dve.wait_ge(lanes_in[q], 16 * s + 16)
                        wait(dve, gathered, done_with(s, q))
                        nc.vector.tensor_scalar(dst1[q % 2][:, 0:n * SLOTS], lanes[q][:, 0:n * SLOTS], lane_no[:, 0:1], None,
                                                ALU.is_equal).then_inc(dst1_ready, 1)
                        wait(dve, scattered, done_with(s, q))
                        nc.vector.tensor_tensor(src1[q % 2][:, 0:n // 2, :], across(iota[:], n // 2),
                                                along(src_lane[:, q * QC // 2:q * QC // 2 + n // 2, bass.ds(s, 1)]
                                                      .rearrange("p j o -> p (j o)"), P),
                                                ALU.is_equal).then_inc(src1_ready, 1)

                    def current(k, b):
                        if r == 0:
                            dve.wait_ge(sums4_ready, k + 1)
                            plain(nc.vector.tensor_reduce(h[:, bass.ds(k, 1), H:H + 1],
                                                          sums4[b][:, 0:3].rearrange("p (o f) -> p o f", o=1),
                                                          AX.X, ALU.add)).then_inc(attr_sum, 1)
                            plain(nc.vector.tensor_copy(degree[:, bass.ds(k, 1)], sums4[b][:, 3:4])).then_inc(attr_sum, 1)
                            dve.wait_ge(attr_sum, 2 * k + 2)
                        wait(dve, turned, k - 1)
                        plain(nc.vector.tensor_copy(hcur[b][:].rearrange("p (o f) -> p o f", o=1),
                                                    h[:, bass.ds(k, 1), :])).then_inc(cur_ready, 1)

                    def gate_inputs(k, b):
                        dve.wait_ge(gates_ready, k + 1)
                        nc.vector.tensor_copy(gi[b][:], ps_gates[:, 0:G]).then_inc(gi_half, 1)
                        dve.wait_ge(gi_half, k + 1)
                        nc.vector.scalar_tensor_tensor(out=gi[b][:], in0=ps_gates[:, 4 * H:4 * H + G],
                                                       scalar=degree[:, bass.ds(k, 1)], in1=gi[b][:],
                                                       op0=ALU.mult, op1=ALU.add).then_inc(gi_ready, 1)

                    def tanh_inputs(k, b):
                        dve.wait_ge(rz_ready, k + 1)
                        nc.vector.tensor_tensor(tn[b][:], rz[b][:, 0:H], ps_gates[:, G:4 * H], ALU.mult).then_inc(tn_half, 1)
                        dve.wait_ge(tn_half, k + 1)
                        nc.vector.tensor_tensor(tn[b][:], tn[b][:], gi[b][:, 2 * H:G], ALU.add).then_inc(tn_ready, 1)

                    def mix(k, b):
                        dve.wait_ge(cand_ready, k + 1)
                        nc.vector.tensor_tensor(tn[b][:], hcur[b][:, 0:H], cand[b][:], ALU.subtract).then_inc(mixed, 1)
                        dve.wait_ge(mixed, 2 * k + 1)
                        nc.vector.tensor_tensor(tn[b][:], tn[b][:], rz[b][:, H:2 * H], ALU.mult).then_inc(mixed, 1)
                        dve.wait_ge(mixed, 2 * k + 2)
                        nc.vector.tensor_tensor(h[:, bass.ds(k, 1), 0:H], tn[b][:].rearrange("p (o f) -> p o f", o=1),
                                                cand[b][:].rearrange("p (o f) -> p o f", o=1), ALU.add).then_inc(h_new, 1)

                    nc.vector.memset(nothing[:], 0.0)
                    for k in range(4):
                        ins = nc.vector.memset(rows[k][:], 0.0)
                    ins.then_inc(rows_zero, 1)

                    def body(s, b, half):
                        one_hots(s, 0)
                        if past(s, 2):
                            tanh_inputs(s - 2, b)
                        one_hots(s, 1)
                        if past(s, 2):
                            mix(s - 2, b)
                        if past(s, 1):
                            current(s - 1, 1 - b)
                        one_hots(s, 2)
                        one_hots(s, 3)
                        if past(s, 1):
                            gate_inputs(s - 1, 1 - b)

                    in_pairs(dve, NT, body)
                    b = (NT - 1) % 2
                    tanh_inputs(NT - 2, 1 - b)
                    mix(NT - 2, 1 - b)
                    current(NT - 1, b)
                    gate_inputs(NT - 1, b)
                    tanh_inputs(NT - 1, b)
                    mix(NT - 1, b)
                    dve.wait_ge(h_new, NT)

        def general_round(r, scope):
            src_sb = sb("src_sb", [P, ET], I32, scope=scope)
            dst_sb = sb("dst_sb", [P, ET], I32, scope=scope)
            attr_sb = sb("attr_sb", [P, ET], scope=scope)
            src_now = sb("src_now", [P, 1], I32, scope=scope)
            dst_now = sb("dst_now", [P, 1], I32, scope=scope)
            put_at = sb("put_at", [P, 1], I32, scope=scope)
            srcf = sb("srcf", [P, 1], scope=scope)
            payload = sb("payload", [P, HA], scope=scope)
            before = sb("before", [P, HA], scope=scope)
            after = sb("after", [P, HA], scope=scope)
            same = sb("same", [P, P], scope=scope)
            dup = sb("dup", [P, P], scope=scope)
            ndup = sb("ndup", [P, 1], scope=scope)
            putf = sb("putf", [P, 1], scope=scope)
            sums = [sb(f"sums{b}", [P, HA], scope=scope) for b in range(2)]
            hcur, sumT, hT, gi, rz, tn, cand = gru_buffers(scope)
            ps_a = ps("ps_a", [P, 512], scope=scope)
            ps_b = ps("ps_b", [P, 512], scope=scope)
            ps_T = ps("ps_T", [P, 2 * P], scope=scope)
            ps_gates = [ps(f"ps_gates{b}", [P, 512], scope=scope) for b in range(2)]
            edges_in = sem(f"edges_in{r}")
            stored = sem(f"stored{r}")
            now_ready = sem(f"now_ready{r}")
            h_got = sem(f"h_got{r}")
            before_got = sem(f"before_got{r}")
            srcT_ready = sem(f"srcT_ready{r}")
            put_ready = sem(f"put_ready{r}")
            group_sum = sem(f"group_sum{r}")
            after_ready = sem(f"after_ready{r}")
            put_done = sem(f"put_done{r}")
            dve_edge = sem(f"dve_edge{r}")
            N_OWN = 6

            with nc.Block() as block:
                @only(block.sync, GENERAL_PATH)
                def _(sp):
                    with nc.allow_non_contiguous_dma(reason="rows of nodes"):
                        sp.dma_start(src_sb[:], src.rearrange("(p t) -> p t", p=P)).then_inc(edges_in, 16)
                        sp.dma_start(dst_sb[:], dst.rearrange("(p t) -> p t", p=P)).then_inc(edges_in, 16)
                        sp.dma_start(attr_sb[:], attr.rearrange("(p t) o -> p (t o)", p=P)).then_inc(edges_in, 16)
                        sp.dma_start(h_dram.rearrange("(t p) f -> p t f", p=P), h[:, :, 0:H]).then_inc(stored, 16)
                        sp.dma_start(sums_dram.rearrange("(t p) f -> p t f", p=P),
                                     zeros[:].rearrange("p (o f) -> p o f", o=1).broadcast_to([P, NT, HA])).then_inc(put_done, 16)
                    sp.wait_ge(stored, 16)
                    sp.wait_ge(put_done, 16)

                @only(block.gpsimd, GENERAL_PATH)
                def _(pool):
                    pool.wait_ge(stored, 16)
                    last_node = pool.to_reg(N - 1)
                    with pool.Fori(0, ET) as i:
                        pool.wait_ge(now_ready, 3 * i + 3)
                        nc.gpsimd.indirect_dma_start(
                            out=payload[:, 0:H], out_offset=None, in_=h_dram,
                            in_offset=bass.IndirectOffsetOnAxis(ap=dst_now[:], axis=0)).wait_op(stored, 16, 'sem-ge').then_inc(h_got, 16)
                        pool.wait_ge(put_done, 16 * i + 16)
                        nc.gpsimd.indirect_dma_start(
                            out=before[:], out_offset=None, in_=sums_dram,
                            in_offset=bass.IndirectOffsetOnAxis(ap=src_now[:], axis=0)).wait_op(stored, 16, 'sem-ge').then_inc(before_got, 16)
                        pool.wait_ge(put_ready, i + 1)
                        pool.wait_ge(after_ready, i + 1)
                        nc.gpsimd.indirect_dma_start(
                            out=sums_dram, out_offset=bass.IndirectOffsetOnAxis(ap=put_at[:], axis=0),
                            in_=after[:], in_offset=None, bounds_check=last_node, oob_is_err=False).wait_op(stored, 16, 'sem-ge').then_inc(put_done, 16)
                    pool.wait_ge(put_done, 16 * ET + 16)

                @only(block.tensor, GENERAL_PATH)
                def _(te):
                    with te.Fori(0, ET) as i:
                        te.wait_ge(now_ready, 3 * i + 3)
                        nc.tensor.transpose(ps_a[:, 0:P], srcf[:].broadcast_to([P, P]), ident[:]).then_inc(srcT_ready, 1)
                        te.wait_ge(put_ready, i + 1)
                        te.wait_ge(h_got, 16 * i + 16)
                        nc.tensor.matmul(ps_b[:, 0:HA], same[:], payload[:], start=True, stop=True).then_inc(group_sum, 1)

                @only(block.vector, GENERAL_PATH)
                def _(dve):
                    dve.wait_ge(edges_in, 48)
                    nc.vector.memset(payload[:, HA - 1:HA], 1.0)
                    with dve.Fori(0, ET) as i:
                        dve.wait_ge(put_done, 16 * i + 16)
                        nc.vector.tensor_copy(dst_now[:], dst_sb[:, bass.ds(i, 1)]).then_inc(now_ready, 1)
                        nc.vector.tensor_copy(src_now[:], src_sb[:, bass.ds(i, 1)])
                        nc.vector.tensor_copy(payload[:, H:H + 1], attr_sb[:, bass.ds(i, 1)]).then_inc(now_ready, 1)
                        nc.vector.tensor_copy(srcf[:], src_sb[:, bass.ds(i, 1)]).then_inc(now_ready, 1)
                        dve.wait_ge(now_ready, 3 * i + 3)
                        dve.wait_ge(srcT_ready, i + 1)
                        nc.vector.tensor_scalar(same[:], ps_a[:, 0:P], srcf[:, 0:1], None, ALU.is_equal).then_inc(dve_edge, 1)
                        dve.wait_ge(dve_edge, N_OWN * i + 1)
                        nc.vector.tensor_tensor(dup[:], same[:], earlier[:], ALU.mult).then_inc(dve_edge, 1)
                        dve.wait_ge(dve_edge, N_OWN * i + 2)
                        nc.vector.tensor_reduce(ndup[:], dup[:], AX.X, ALU.add).then_inc(dve_edge, 1)
                        dve.wait_ge(dve_edge, N_OWN * i + 3)
                        nc.vector.tensor_scalar(ndup[:], ndup[:], 1.0, SKIP, ALU.min, ALU.mult).then_inc(dve_edge, 1)
                        dve.wait_ge(dve_edge, N_OWN * i + 4)
                        nc.vector.tensor_tensor(putf[:], ndup[:], srcf[:], ALU.add).then_inc(dve_edge, 1)
                        dve.wait_ge(dve_edge, N_OWN * i + 5)
                        nc.vector.tensor_copy(put_at[:], putf[:]).then_inc(put_ready, 1)
                        dve.wait_ge(group_sum, i + 1)
                        dve.wait_ge(before_got, 16 * i + 16)
                        nc.vector.tensor_tensor(after[:], before[:], ps_b[:, 0:HA], ALU.add).then_inc(after_ready, 1)
                        nc.vector.tensor_copy(ndup[:], ndup[:]).then_inc(dve_edge, 1)

            sums_got = [sem(f"sums_got{r}_{b}") for b in range(2)]
            cur_ready = sem(f"cur_ready{r}")
            T_turned = sem(f"T_turned{r}")
            T_ready = sem(f"T_ready{r}")
            gates_ready = sem(f"gates_ready{r}")
            gi_ready = sem(f"gi_ready{r}")
            rz_ready = sem(f"rz_ready{r}")
            tn_ready = sem(f"tn_ready{r}")
            cand_ready = sem(f"cand_ready{r}")
            h_new = sem(f"h_new{r}")
            dve_gru = sem(f"dve_gru{r}")

            with nc.Block() as block:
                @only(block.sync, GENERAL_PATH)
                def _(sp):
                    def body(k, b, half):
                        wait(sp, h_new, 2 * half)
                        sp.dma_start(sums[b][:], sums_dram[bass.ds(k * P, P), :]).then_inc(sums_got[b], 16)

                    in_pairs(sp, NT, body)

                @only(block.tensor, GENERAL_PATH)
                def _(te):
                    def body(k, b, half):
                        te.wait_ge(cur_ready, k + 1)
                        wait(te, T_ready, 2 * k)
                        nc.tensor.transpose(ps_T[0:HA, P:2 * P], hcur[b][:], ident[:])
                        nc.tensor.transpose(ps_T[0:H, 0:P], sums[b][:, 0:H], ident[:]).then_inc(T_turned, 1)
                        te.wait_ge(T_ready, 2 * k + 2)
                        wait(te, h_new, 2 * half)
                        nc.tensor.matmul(ps_gates[b][:, 0:4 * H + G], hT[b][:], w_node[:, r, :], start=True, stop=False)
                        nc.tensor.matmul(ps_gates[b][:, 0:G], sumT[b][0:H, :], w_sum[0:H, r, :], start=False,
                                         stop=True).then_inc(gates_ready, 1)

                    in_pairs(te, NT, body)

                @only(block.scalar, GENERAL_PATH)
                def _(act):
                    def body(k, b, half):
                        act.wait_ge(T_turned, k + 1)
                        wait(act, gates_ready, 2 * half)
                        nc.scalar.activation(sumT[b][0:H, :], ps_T[0:H, 0:P], ACT.Copy).then_inc(T_ready, 1)
                        nc.scalar.activation(hT[b][:], ps_T[0:HA, P:2 * P], ACT.Copy).then_inc(T_ready, 1)
                        act.wait_ge(gi_ready, k + 1)
                        nc.scalar.activation(rz[b][:], gi[b][:, 0:2 * H], ACT.Sigmoid).then_inc(rz_ready, 1)
                        act.wait_ge(tn_ready, k + 1)
                        nc.scalar.activation(cand[b][:], tn[b][:], ACT.Tanh).then_inc(cand_ready, 1)

                    in_pairs(act, NT, body)

                @only(block.vector, GENERAL_PATH)
                def _(dve):
                    def body(k, b, half):
                        own = lambda n: 5 * k + n
                        dve.wait_ge(sums_got[b], 16 * half + 16)
                        nc.vector.tensor_copy(h[:, bass.ds(k, 1), H:H + 1],
                                              sums[b][:, H:H + 1].rearrange("p (o f) -> p o f", o=1)).then_inc(dve_gru, 1)
                        dve.wait_ge(dve_gru, own(1))
                        nc.vector.tensor_copy(hcur[b][:].rearrange("p (o f) -> p o f", o=1),
                                              h[:, bass.ds(k, 1), :]).then_inc(cur_ready, 1)
                        dve.wait_ge(gates_ready, k + 1)
                        nc.vector.tensor_copy(gi[b][:], ps_gates[b][:, 0:G]).then_inc(dve_gru, 1)
                        dve.wait_ge(dve_gru, own(2))
                        nc.vector.scalar_tensor_tensor(out=gi[b][:], in0=ps_gates[b][:, 4 * H:4 * H + G],
                                                       scalar=sums[b][:, H + 1:HA], in1=gi[b][:],
                                                       op0=ALU.mult, op1=ALU.add).then_inc(gi_ready, 1)
                        dve.wait_ge(gi_ready, k + 1)
                        dve.wait_ge(rz_ready, k + 1)
                        nc.vector.tensor_tensor(tn[b][:], rz[b][:, 0:H], ps_gates[b][:, G:4 * H], ALU.mult).then_inc(dve_gru, 1)
                        dve.wait_ge(dve_gru, own(3))
                        nc.vector.tensor_tensor(tn[b][:], tn[b][:], gi[b][:, 2 * H:G], ALU.add).then_inc(tn_ready, 1)
                        dve.wait_ge(cand_ready, k + 1)
                        dve.wait_ge(cur_ready, k + 1)
                        nc.vector.tensor_tensor(tn[b][:], hcur[b][:, 0:H], cand[b][:], ALU.subtract).then_inc(dve_gru, 1)
                        dve.wait_ge(dve_gru, own(4))
                        nc.vector.tensor_tensor(tn[b][:], tn[b][:], rz[b][:, H:2 * H], ALU.mult).then_inc(dve_gru, 1)
                        dve.wait_ge(dve_gru, own(5))
                        nc.vector.tensor_tensor(h[:, bass.ds(k, 1), 0:H], tn[b][:].rearrange("p (o f) -> p o f", o=1),
                                                cand[b][:].rearrange("p (o f) -> p o f", o=1), ALU.add).then_inc(h_new, 1)

                    in_pairs(dve, NT, body)


        for r in range(ROUNDS):
            with ExitStack() as scope:
                sums_round(r, scope)
        for r in range(ROUNDS):
            with ExitStack() as scope:
                general_round(r, scope)

        x_again = sem("x_again")
        added = sem("added")
        result = sem("result")
        wide = sb("wide_again", [P, NT, H])
        with nc.Block() as block:
            @block.sync
            def _(sp):
                with nc.allow_non_contiguous_dma(reason="rows of nodes"):
                    sp.dma_start(wide[:, 0:NT - 1, :], x[0:(NT - 1) * P, :].rearrange("(t p) f -> p t f", p=P)).then_inc(x_again, 16)
                    sp.dma_start(wide[0:TAIL, NT - 1, :], x[(NT - 1) * P:N, :]).then_inc(x_again, 16)
                    sp.wait_ge(added, 2)
                    sp.dma_start(out[0:(NT - 1) * P, :].rearrange("(t p) f -> p t f", p=P), wide[:, 0:NT - 1, :]).then_inc(result, 16)
                    sp.dma_start(out[(NT - 1) * P:N, :], wide[0:TAIL, NT - 1, :]).then_inc(result, 16)
                sp.wait_ge(result, 32)

            @block.vector
            def _(dve):
                dve.wait_ge(x_again, 32)
                nc.vector.tensor_tensor(wide[:, 0:NT - 1, :], wide[:, 0:NT - 1, :], h[:, 0:NT - 1, 0:H], ALU.add).then_inc(added, 1)
                nc.vector.tensor_tensor(wide[0:TAIL, NT - 1, :], wide[0:TAIL, NT - 1, :], h[0:TAIL, NT - 1, 0:H],
                                        ALU.add).then_inc(added, 1)


_INS = ["x", "src", "dst", "edge_weight1", "L0_gnn_msg_W", "L0_gnn_msg_b", "L0_gnn_gru_Wih", "L0_gnn_gru_bih",
        "L0_gnn_gru_Whh", "L0_gnn_gru_bhh"]


def kernel(**inputs):
    import numpy as _np
    import concourse.bacc as _bacc
    from concourse import mybir as _mybir
    from concourse.bass_utils import run_bass_kernel_spmd as _run

    nc = _bacc.Bacc("TRN2", target_bir_lowering=False, num_devices=1)
    arrays, args = {}, []
    for name in _INS:
        a = _np.ascontiguousarray(inputs[name])
        arrays[f"in_{name}_dram"] = a
        args.append(nc.dram_tensor(f"in_{name}_dram", a.shape, _mybir.dt.from_np(a.dtype), kind="ExternalInput").ap())
    out = nc.dram_tensor("out_0_dram", inputs["x"].shape, F32, kind="ExternalOutput").ap()
    build(nc, *args, out)
    r = _run(nc, [arrays], core_ids=[0])
    return r.results[0]["out_0_dram"]
```

```python
from contextlib import ExitStack

import concourse.bass as bass
from concourse import mybir

P = 128
F32 = mybir.dt.float32
F16 = mybir.dt.float16
BF16 = mybir.dt.bfloat16
I32 = mybir.dt.int32
I16 = mybir.dt.int16
U8 = mybir.dt.uint8
ALU = mybir.AluOpType
ACT = mybir.ActivationFunctionType
AX = mybir.AxisListType
EPS = 1e-5
SLOTS = 64
BIG = 2048.0
LO = 2048.0
UJ = 4
NQ = 4
TENSOR_PATH, GENERAL_PATH = 0, 1
PEELED = 4
LAG = 3


class Chain:

    def __init__(self, engine, sem):
        self.engine, self.sem, self.at = engine, sem, 0

    def __call__(self, ins):
        self.at += 1
        ins.then_inc(self.sem, 1)
        self.engine.wait_ge(self.sem, self.at)


def wait(engine, sem, value):
    if not isinstance(value, int) or value > 0:
        engine.wait_ge(sem, value)


def past(i, n):
    return not isinstance(i, int) or i >= n


def in_pairs(engine, n, body):
    for i in range(min(PEELED, n)):
        body(i, i % 2, i // 2)
    if n // 2 > PEELED // 2:
        with engine.Fori(PEELED // 2, n // 2) as i:
            body(2 * i, 0, i)
            body(2 * i + 1, 1, i)
    if n % 2 and n > PEELED:
        body(n - 1, 0, n // 2)


def tiles_per_chunk(tiles, nodes, node_tiles):
    edges = tiles * P
    fits = [k for k in range(1, tiles + 1)
            if tiles % k == 0 and k * P * nodes <= 0.8 * P * edges and k * P <= 0.52 * SLOTS * node_tiles]
    return max(fits)


def split(t, a):
    return t.rearrange("p (a b) -> p a b", a=a)


def along(t, n):
    return t.rearrange("p (a o) -> p a o", o=1).broadcast_to([t.shape[0], t.shape[1], n])


def across(t, n):
    return t.rearrange("p (o b) -> p o b", o=1).broadcast_to([t.shape[0], n, t.shape[1]])


def build(nc, x, src, dst, attr, msg_W, msg_b, Wih, bih, Whh, bhh, out):
    N, H = x.shape
    E = src.shape[0]
    ROUNDS = msg_W.shape[0]
    NT = -(-N // P)
    NP = NT * P
    TAIL = N - (NT - 1) * P
    ET = E // P
    CT = tiles_per_chunk(ET, N, NT)
    C = ET // CT
    TP = -(-CT // 2)
    RP = min(4, CT // 2)
    R0, R1 = CT // 2 * 2 - 2 * RP, CT // 2 * 2
    NG = -(-RP // 2)
    PIECES = [(p0, p1) for p0, p1 in ((-(-TP * k // 4), -(-TP * (k + 1) // 4)) for k in range(4)) if p1 > p0]
    BY_POOL = 2 * len(PIECES) - 1
    J = -(-C // 2)
    NU = -(-J // UJ)
    JP = NU * UJ
    UQ = -(-NU // NQ)
    QC = UQ * UJ * 2
    assert ROUNDS > 1 and JP >= H and C >= NT and 4 * NT <= 512 and J * NT <= C * H and E % P == 0 and H == 64 and NT % 2 == 0 and NU > (NQ - 1) * UQ and UQ >= LAG and N >= P
    HA = H + 2
    G = 3 * H
    SKIP = float(1 << 22)

    def pairs_of(u):
        return range(u * UJ, min(u * UJ + UJ, J))

    SUM_AT, TURN_AT, GATES_AT, SIGMOID_AT, TANH_AT = [min(k, NU - 2) for k in (3, 6, 9, 12, 1)]

    def units_of(q):
        return range(q * UQ, min(q * UQ + UQ, NU))

    with ExitStack() as ctx:
        names_taken = {}

        def fresh(name):
            names_taken[name] = names_taken.get(name, 0) + 1
            return f"{name}_{names_taken[name]}" if names_taken[name] > 1 else name

        def sb(name, shape, dt=F32, scope=ctx):
            return scope.enter_context(nc.sbuf_tensor(fresh(name), shape, dt))

        def ps(name, shape, dt=F32, scope=ctx):
            return scope.enter_context(nc.psum_tensor(fresh(name), shape, dt))

        def sem(name):
            return ctx.enter_context(nc.semaphore(name))

        path_sems = {}

        def path_sem(name):
            if name not in path_sems:
                path_sems[name] = sem(name)
            return path_sems[name]

        def dram(name, shape, dt=F32):
            return nc.dram_tensor(name, shape, dt, kind="Internal").ap()

        def gru_buffers(scope):
            return [[sb(f"{name}{b}", shape, scope=scope) for b in range(2)] for name, shape in
                    (("hcur", [P, HA]), ("sumT", [P, P]), ("hT", [HA, P]), ("gi", [P, G]), ("rz", [P, 2 * H]),
                     ("tn", [P, H]), ("cand", [P, H]))]

        h_dram = dram("h_dram", [NP, H])
        sums_dram = dram("sums_dram", [NP, HA])
        parts_dram = [dram(f"parts_dram{b}", [NP, 2 * H], F16) for b in range(2)]
        lanes_dram = dram("lanes_dram", [NT, NQ * QC * SLOTS], F16)

        h = sb("h", [P, NT, HA])
        ident = sb("ident", [P, P])
        earlier = sb("earlier", [P, P])
        later = sb("later", [P, P])
        lane_no = sb("lane_no", [P, 1])
        lane_no_i = sb("lane_no_i", [P, 1], I32)
        begun = sem("begun")

        def plain(ins):
            return ins.wait_op(begun, 1, "sem-ge")

        ones = sb("ones", [P, P])
        zeros = sb("zeros", [P, HA])
        wmsg = sb("wmsg", [H, ROUNDS, 2 * H + 2])
        wmsg_parts = sb("wmsg_parts", [H, ROUNDS, 2 * H])
        pick = sb("pick", [HA, 2])
        w_sum = sb("w_sum", [P, ROUNDS, G])
        w_node = sb("w_node", [HA, ROUNDS, 4 * H + G])
        iota = sb("iota", [P, P], F16)
        degree = sb("degree", [P, NT])
        at_slot = sb("at_slot", [P, NT, JP], I16)
        src_lane = at_slot[:].bitcast(F16)
        attr_slot = sb("attr_slot", [P, NT, JP])
        rows_now = sb("rows_now", [P, C, 2 * H], F16)
        first = sb("first", [1, C], I32)
        spans = sb("spans", [1, C], I32)
        misfit = sb("misfit", [1, 1], I32)

        padded = sem("padded")
        edges_in = sem("edges_in")
        const = sem("const")
        rows_in = sem("rows_in")
        inputs = sem("inputs")
        cleared = sem("cleared")
        var_ready = sem("var_ready")
        std_ready = sem("std_ready")
        turned = sem("turned")
        gate_w = sem("gate_w")
        biases = sem("biases")
        folded = sem("folded")
        fold_used = sem("fold_used")
        parts_ready = sem("parts_ready")
        dve_own = sem("dve_own")
        high_ready = sem("high_ready")
        rest_ready = sem("rest_ready")
        low_ready = sem("low_ready")
        parts_out = sem("parts_out")
        N_CONST, N_INPUTS, N_BIASES = 9, 16 * (2 + 2 * ROUNDS), 16 * 3 * ROUNDS

        loop_scope = ctx.enter_context(ExitStack())
        attr_e = sb("attr_e", [P, C, 2 * TP], scope=loop_scope)
        code = sb("code", [P, C, 2 * TP], scope=loop_scope)
        tile_e = sb("tile_e", [P, C, 2 * TP], F16, scope=loop_scope)
        twins = sb("twins", [P, C, CT], U8, scope=loop_scope)
        worst = sb("worst", [P, CT], scope=loop_scope)
        stray = sb("stray", [P, 2], scope=loop_scope)
        edge_scope = ctx.enter_context(ExitStack())
        src_i = sb("src_i", [P, C, CT], I32, scope=edge_scope)
        dst_i = sb("dst_i", [P, C, CT], I32, scope=edge_scope)
        prep_scope = ctx.enter_context(ExitStack())
        wih = sb("wih", [H, 3, ROUNDS, H], scope=prep_scope)
        whh = sb("whh", [H, 3, ROUNDS, H], scope=prep_scope)
        wihT = sb("wihT", [H, ROUNDS, G], scope=prep_scope)
        bias = sb("bias", [HA, ROUNDS, 4 * H], scope=prep_scope)
        wide = sb("wide", [P, NT, H], scope=prep_scope)
        total, mean, var, std, newton, rstd = [sb(n, [P, NT], scope=prep_scope)
                                               for n in ("total", "mean", "var", "std", "newton", "rstd")]
        iota_i = sb("iota_i", [P, P], I32, scope=prep_scope)
        ps_a = ps("ps_a", [P, 512], scope=prep_scope)
        ps_b = ps("ps_b", [P, 512], scope=prep_scope)

        with nc.Block() as block:
            @block.sync
            def _(sp):
                with nc.allow_non_contiguous_dma(reason="small weights"):
                    sp.wait_ge(padded, 1)
                    sp.dma_start(h[:, 0:NT - 1, 0:H],
                                 x[0:(NT - 1) * P, :].rearrange("(t p) f -> p t f", p=P)).then_inc(rows_in, 16)
                    sp.dma_start(h[0:TAIL, NT - 1, 0:H], x[(NT - 1) * P:N, :]).then_inc(rows_in, 16)
                    sp.dma_start(dst_i[:], dst.rearrange("(c p t) -> p c t", p=P, t=CT)).then_inc(edges_in, 16)
                    sp.dma_start(src_i[:], src.rearrange("(c p t) -> p c t", p=P, t=CT)).then_inc(edges_in, 16)
                    sp.dma_start(attr_e[:, :, 0:CT], attr.rearrange("(c p t) o -> p c (t o)", p=P, t=CT)).then_inc(edges_in, 16)
                    sp.wait_ge(edges_in, 48)

            @block.gpsimd
            def _(pool):
                nc.gpsimd.memset(h[:, NT - 1, 0:H], 0.0).then_inc(padded, 1)
                nc.gpsimd.iota(lane_no_i[:], pattern=[[0, 1]], base=0, channel_multiplier=1).then_inc(const, 1)
                nc.gpsimd.iota(iota_i[:], pattern=[[1, P]], base=0, channel_multiplier=0).then_inc(const, 1)
                nc.gpsimd.memset(zeros[:], 0.0).then_inc(const, 1)
                nc.gpsimd.memset(ones[:], 1.0).then_inc(const, 1)
                pool.wait_ge(const, 4)
                nc.gpsimd.affine_select(out=ident[:], in_=ones[:], compare_op=ALU.is_equal, fill=0.0, base=0,
                                        pattern=[[-1, P]], channel_multiplier=1).then_inc(const, 1)
                nc.gpsimd.affine_select(out=earlier[:], in_=ones[:], compare_op=ALU.is_gt, fill=0.0, base=0,
                                        pattern=[[-1, P]], channel_multiplier=1).then_inc(const, 1)
                nc.gpsimd.affine_select(out=later[:], in_=ones[:], compare_op=ALU.is_gt, fill=0.0, base=0,
                                        pattern=[[1, P]], channel_multiplier=-1).then_inc(const, 1)
                nc.gpsimd.affine_select(out=pick[:, 0:1], in_=ones[0:HA, 0:1], compare_op=ALU.is_equal, fill=0.0,
                                        base=-H, pattern=[[0, 1]], channel_multiplier=1).then_inc(const, 1)
                nc.gpsimd.affine_select(out=pick[:, 1:2], in_=ones[0:HA, 0:1], compare_op=ALU.not_equal, fill=0.0,
                                        base=-H, pattern=[[0, 1]], channel_multiplier=1).then_inc(const, 1)

            @block.tensor
            def _(te):
                te.wait_ge(inputs, N_INPUTS)
                te.wait_ge(const, N_CONST)
                for r in range(ROUNDS):
                    if r:
                        te.wait_ge(gate_w, 3 * r)
                    for g in range(3):
                        nc.tensor.transpose(ps_a[0:H, g * H:(g + 1) * H], wih[:, g, r, :], ident[0:H, 0:H])
                        last = nc.tensor.transpose(ps_b[0:H, g * H:(g + 1) * H], whh[:, g, r, :], ident[0:H, 0:H])
                    last.then_inc(turned, 1)
                te.wait_ge(gate_w, 3 * ROUNDS)
                te.wait_ge(parts_ready, 2)
                for r in range(ROUNDS):
                    if r:
                        te.wait_ge(fold_used, 3 * r)
                    nc.tensor.matmul(ps_a[:, 0:G], wmsg_parts[:, r, :], wihT[:, r, :], start=True, stop=True)
                    nc.tensor.matmul(ps_b[0:HA, 0:G], wmsg[:, r, H:2 * H + 2], wihT[:, r, :], start=True,
                                     stop=True).then_inc(folded, 1)

            @block.scalar
            def _(act):
                with nc.allow_non_contiguous_dma(reason="small weights"):
                    act.dma_start(wmsg[:, :, 0:2 * H + 1], msg_W.rearrange("r m k -> m r k")).then_inc(inputs, 16)
                    act.dma_start(wmsg[:, :, 2 * H + 1:2 * H + 2],
                                  msg_b.rearrange("r (m o) -> m r o", o=1)).then_inc(inputs, 16)
                    for r in range(ROUNDS):
                        act.dma_start(wih[:, :, r, :], Wih[r].rearrange("(g m) k -> m g k", g=3)).then_inc(inputs, 16)
                        act.dma_start(whh[:, :, r, :], Whh[r].rearrange("(g m) k -> m g k", g=3)).then_inc(inputs, 16)
                    act.wait_ge(cleared, 2)
                    for r in range(ROUNDS):
                        act.dma_start(w_node[HA - 1:HA, r, 0:G], bih[r:r + 1, :]).then_inc(biases, 16)
                        act.dma_start(bias[HA - 1:HA, r, 0:2 * H], bhh[r:r + 1, 0:2 * H]).then_inc(biases, 16)
                        act.dma_start(bias[HA - 1:HA, r, 3 * H:4 * H], bhh[r:r + 1, 2 * H:G]).then_inc(biases, 16)
                act.wait_ge(var_ready, 1)
                nc.scalar.activation(std[:], var[:], ACT.Sqrt).then_inc(std_ready, 1)
                act.wait_ge(cleared, 2)
                for r in range(ROUNDS):
                    act.wait_ge(turned, r + 1)
                    nc.scalar.activation(wihT[:, r, :], ps_a[0:H, 0:G], ACT.Copy).then_inc(gate_w, 1)
                    nc.scalar.activation(w_node[0:H, r, 0:2 * H], ps_b[0:H, 0:2 * H], ACT.Copy).then_inc(gate_w, 1)
                    nc.scalar.activation(w_node[0:H, r, 3 * H:4 * H], ps_b[0:H, 2 * H:G], ACT.Copy).then_inc(gate_w, 1)

            @block.vector
            def _(dve):
                step = Chain(dve, dve_own)
                rows = h[:, :, 0:H]

                def per_row(t):
                    return t[:].rearrange("p (t o) -> p t o", o=1).broadcast_to([P, NT, H])

                nc.vector.memset(w_node[:], 0.0).then_inc(cleared, 1)
                nc.vector.memset(bias[:], 0.0).then_inc(cleared, 1)
                step(nc.vector.memset(h[:, :, H:H + 1], 0.0))
                step(nc.vector.memset(h[:, :, H + 1:HA], 1.0))
                dve.wait_ge(rows_in, 32)
                dve.wait_ge(const, N_CONST)
                nc.vector.tensor_copy(iota[:], iota_i[:])
                nc.vector.tensor_copy(lane_no[:], lane_no_i[:]).then_inc(begun, 1)
                step(nc.vector.tensor_reduce(total[:], rows, AX.X, ALU.add))
                step(nc.vector.tensor_scalar(mean[:], total[:], 1.0 / H, None, ALU.mult))
                step(nc.vector.tensor_tensor(rows, rows, per_row(mean), ALU.subtract))
                step(nc.vector.tensor_tensor(wide[:], rows, rows, ALU.mult))
                step(nc.vector.tensor_reduce(total[:], wide[:], AX.X, ALU.add))
                nc.vector.tensor_scalar(var[:], total[:], 1.0 / H, EPS, ALU.mult, ALU.add).then_inc(var_ready, 1)
                dve.wait_ge(std_ready, 1)
                step(nc.vector.reciprocal(newton[:], std[:]))
                step(nc.vector.tensor_tensor(newton[:], newton[:], var[:], ALU.mult))
                step(nc.vector.tensor_tensor(newton[:], newton[:], std[:], ALU.add))
                step(nc.vector.tensor_scalar(newton[:], newton[:], 0.5, None, ALU.mult))
                step(nc.vector.reciprocal(rstd[:], newton[:]))
                step(nc.vector.tensor_tensor(rows, rows, per_row(rstd), ALU.mult))
                nc.vector.tensor_scalar(rows, rows, 0.0, None, ALU.max)
                dve.wait_ge(inputs, N_INPUTS)
                nc.vector.tensor_copy(wmsg_parts[:, :, 0:H], wmsg[:, :, 0:H]).then_inc(parts_ready, 1)
                nc.vector.tensor_scalar(wmsg_parts[:, :, H:2 * H], wmsg[:, :, 0:H], 1.0 / LO, None,
                                        ALU.mult).then_inc(parts_ready, 1)
                dve.wait_ge(gate_w, 3 * ROUNDS)
                dve.wait_ge(biases, N_BIASES)
                for r in range(ROUNDS):
                    step(nc.vector.tensor_tensor(w_node[:, r, 0:4 * H], w_node[:, r, 0:4 * H], bias[:, r, :], ALU.add))
                    dve.wait_ge(folded, r + 1)
                    nc.vector.tensor_copy(w_sum[:, r, :], ps_a[:, 0:G]).then_inc(fold_used, 1)
                    nc.vector.scalar_tensor_tensor(out=w_node[:, r, 0:G], in0=ps_b[0:HA, 0:G], scalar=pick[:, 0:1],
                                                   in1=w_node[:, r, 0:G], op0=ALU.mult, op1=ALU.add).then_inc(fold_used, 1)
                    nc.vector.tensor_scalar(w_node[:, r, 4 * H:4 * H + G], ps_b[0:HA, 0:G], pick[:, 1:2], None,
                                            ALU.mult).then_inc(fold_used, 1)

        prep_scope.close()

        part_i = sb("part_i", [P, C, CT], I32, scope=edge_scope)
        lane_f = sb("lane_f", [P, C, CT], scope=edge_scope)
        CE = C + C % 2
        tile_T = sb("tile_T", [P, CT, CE], F16, scope=edge_scope)
        twins_T = (lane_f[:].rearrange("p c t -> p (c t)").bitcast(F16)[:, 0:CT * CE]
                   .rearrange("p (t c) -> p t c", t=CT))
        alike = sb("alike", [P, CT, CE], F16, scope=edge_scope)
        firstf = sb("firstf", [1, C], scope=edge_scope)
        lastf = sb("lastf", [1, C], scope=edge_scope)
        first_all = sb("first_all", [P, C], scope=edge_scope)
        ps_first = ps("ps_first", [P, 512], scope=edge_scope)

        parts = rows_now[:, 0:NT, :]
        rest = attr_slot[:].rearrange("p s j -> p (s j)")[:, 0:NT * H].rearrange("p (t f) -> p t f", t=NT)
        firstf_ready = sem("firstf_ready")
        first_ps = sem("first_ps")
        dve_edges = sem("dve_edges")
        with nc.Block() as block:
            @block.scalar
            def _(act):
                nc.scalar.activation(parts[:, :, 0:H], h[:, :, 0:H], ACT.Copy).then_inc(high_ready, 1)
                act.wait_ge(rest_ready, 1)
                nc.scalar.activation(parts[:, :, H:2 * H], rest, ACT.Copy, scale=LO).then_inc(low_ready, 1)

            @block.gpsimd
            def _(pool):
                pool.wait_ge(high_ready, 1)
                nc.gpsimd.tensor_tensor(rest, h[:, :, 0:H], parts[:, :, 0:H], ALU.subtract).then_inc(rest_ready, 1)

            @block.sync
            def _(sp):
                sp.wait_ge(low_ready, 1)
                with nc.allow_non_contiguous_dma(reason="rows of nodes"):
                    sp.dma_start(parts_dram[0].rearrange("(t p) f -> p t f", p=P), parts).then_inc(parts_out, 16)
                sp.wait_ge(parts_out, 16)

            @block.tensor
            def _(te):
                te.wait_ge(firstf_ready, 1)
                nc.tensor.matmul(ps_first[:, 0:C], ones[0:1, :], firstf[:], start=True, stop=True).then_inc(first_ps, 1)

            @block.vector
            def _(dve):
                step = Chain(dve, dve_edges)
                dve.wait_ge(edges_in, 48)
                step(nc.vector.tensor_copy(firstf[:], dst_i[0:1, :, 0]))
                step(nc.vector.tensor_scalar(firstf[:], firstf[:], float(NP - P), 0.0, ALU.min, ALU.max))
                nc.vector.tensor_copy(first[:], firstf[:]).then_inc(firstf_ready, 1)
                dve.wait_ge(firstf_ready, 1)
                step(nc.vector.tensor_scalar(lastf[:], firstf[:], float(2 * P - 1), None, ALU.add))
                step(nc.vector.tensor_copy(spans[:], lastf[:]))
                step(nc.vector.tensor_scalar(spans[:], spans[:], 7, None, ALU.arith_shift_right))
                dve.wait_ge(first_ps, 1)
                step(nc.vector.tensor_copy(first_all[:], ps_first[:, 0:C]))
                step(nc.vector.tensor_copy(lane_f[:], dst_i[:]))
                step(nc.vector.tensor_tensor(lane_f[:], lane_f[:], along(first_all[:], CT), ALU.subtract))
                step(nc.vector.tensor_reduce(stray[:, 0:1], lane_f[:], AX.XY, ALU.max))
                step(nc.vector.tensor_reduce(stray[:, 1:2], lane_f[:], AX.XY, ALU.min))
                step(nc.vector.tensor_scalar(part_i[:], src_i[:], P - 1, None, ALU.bitwise_and))
                if CT % 2:
                    step(nc.vector.memset(code[:, :, CT:], 0.0))
                    step(nc.vector.memset(attr_e[:, :, CT:], 0.0))
                    step(nc.vector.memset(tile_e[:, :, CT:], -1.0))
                step(nc.vector.tensor_scalar(lane_f[:], lane_f[:], 1.0, None, ALU.add))
                step(nc.vector.tensor_copy(code[:, :, 0:CT], part_i[:]))
                step(nc.vector.scalar_tensor_tensor(out=code[:, :, 0:CT], in0=code[:, :, 0:CT], scalar=float(P),
                                                    in1=lane_f[:], op0=ALU.mult, op1=ALU.add))
                step(nc.vector.tensor_scalar(part_i[:], src_i[:], 7, None, ALU.arith_shift_right))
                if C % 2:
                    step(nc.vector.memset(tile_T[:, :, C:], 0.0))
                step(nc.vector.tensor_copy(tile_T[:, :, 0:C], part_i[:].rearrange("p c t -> p t c")))
                step(nc.vector.tensor_copy(tile_e[:, :, 0:CT], part_i[:]))
                step(nc.vector.memset(twins_T, 0.0))
                for d in range(1, CT):
                    step(nc.vector.tensor_tensor(alike[:, d:, :], tile_T[:, d:, :], tile_T[:, 0:CT - d, :], ALU.is_equal))
                    step(nc.vector.tensor_tensor(twins_T[:, d:, :], twins_T[:, d:, :], alike[:, d:, :], ALU.add))
                step(nc.vector.tensor_copy(twins[:], twins_T[:, :, 0:C].rearrange("p t c -> p c t")))
                step(nc.vector.memset(worst[:], 0.0))
                step(nc.vector.memset(at_slot[:], 0))
                dve.wait_ge(low_ready, 1)
                step(nc.vector.memset(attr_slot[:], 0.0))
        edge_scope.close()

        iota_tiles = sb("iota_tiles", [P, NT, 2], F16, scope=loop_scope)
        iota_slots = sb("iota_slots", [P, SLOTS, 2], F16, scope=loop_scope)
        below_big = sb("below_big", [P, 1], scope=loop_scope)
        lift = sb("lift", [P, P], F16, scope=loop_scope)
        unit16 = sb("unit16", [P, P], F16, scope=loop_scope)
        before16 = sb("before16", [P, P], F16, scope=loop_scope)
        pair = range(2)
        onehot = [sb(f"onehot{b}", [P, TP, NT, 2], F16, scope=loop_scope) for b in pair]
        slot1 = [sb(f"slot1{b}", [P, TP, SLOTS, 2], F16, scope=loop_scope) for b in pair]
        onehot32 = [sb(f"onehot32{b}", [P, TP, 2, NT], scope=loop_scope) for b in pair]
        lanes_before = [sb(f"lanes_before{b}", [P, NT], F16, scope=loop_scope) for b in pair]
        top = [sb(f"top{b}", [P, CT], scope=loop_scope) for b in pair]
        rank = [sb(f"rank{b}", [P, 2 * TP], F16, scope=loop_scope) for b in pair]
        placed_vals = [sb(f"placed_vals{b}", [P, 2 * TP, 2, SLOTS], scope=loop_scope) for b in pair]
        unused = sb("unused", [P, CT - (R1 - R0), NT], BF16, scope=loop_scope)
        ps_before_bank = [ps(f"ps_before{b}", [P, 512], scope=loop_scope) for b in pair]
        ps_count_bank = [ps(f"ps_count{b}", [P, 512], scope=loop_scope) for b in pair]
        ps_slots_bank = [ps(f"ps_slots{b}", [P, 512], scope=loop_scope) for b in pair]

        ps_check = ps("ps_check", [P, 512], scope=loop_scope)
        ps_before = [t[:, 0:NT] for t in ps_before_bank]
        ps_count = [t[:, 0:4 * NT].rearrange("p (t s) -> p t s", t=4) for t in ps_count_bank]
        ps_slots = [t[:, 0:NT] for t in ps_slots_bank]

        mats = sem("mats")
        onehot_ready = sem("onehot_ready")
        onehot32_ready = sem("onehot32_ready")
        before_ps = sem("before_ps")
        before_ready = sem("before_ready")
        count_ps = sem("count_ps")
        top_ready = sem("top_ready")
        top_act = sem("top_act")
        rank_ready = sem("rank_ready")
        slot_ready = sem("slot_ready")
        made = sem("made")
        last_codes = sem("last_codes")
        placed_ready = sem("placed_ready")
        slots_ps = sem("slots_ps")
        slots_kept = sem("slots_kept")
        worst_ready = sem("worst_ready")

        windows_in = sem("windows_in")

        def product(c, b, p0, p1, v):
            values = (code, attr_e)[v]
            return (placed_vals[b][:, 2 * p0:2 * p1, v, :].rearrange("p (g k) s -> p g k s", k=2),
                    slot1[b][:, p0:p1, :, :].rearrange("p g s k -> p g k s"),
                    values[:, bass.ds(c, 1), 2 * p0:2 * p1].rearrange("p (o s) (g k) -> p (o g) k s", s=1, k=2)
                    .broadcast_to([P, p1 - p0, 2, SLOTS]))

        def more_after(c):
            return not (isinstance(c, int) and c == C - 1)

        def group(g):
            return range(R0 // 2 + 2 * g, min(R0 // 2 + 2 * g + 2, R1 // 2))

        with nc.Block() as block:
            @block.sync
            def _(sp):
                with sp.Fori(0, C) as c:
                    at = sp.value_load(first[0:1, bass.ds(c, 1)], min_val=0, max_val=NP - P)
                    sp.dma_start(rows_now[:, bass.ds(c, 1), :].rearrange("p o f -> p (o f)"),
                                 parts_dram[0][bass.ds(at, P), :]).then_inc(windows_in, 16)
                sp.wait_ge(windows_in, 16 * C)

            @block.tensor
            def _(te):
                te.wait_ge(mats, 4)

                def place(c, b):
                    te.wait_ge(onehot32_ready, c + 1)
                    wait(te, slots_kept, 2 * (c - 1))
                    for n, (p0, p1) in enumerate(PIECES):
                        if n < len(PIECES) - 1:
                            te.wait_ge(placed_ready, BY_POOL * c + 2 * n + 2)
                        else:
                            te.wait_ge(placed_ready, BY_POOL * (c + 1))
                            te.wait_ge(last_codes, c + 1)
                        for t in range(2 * p0, min(2 * p1, CT)):
                            last = nc.tensor.matmul(ps_slots[b][:], placed_vals[b][:, t, :, :].rearrange("p v s -> p (v s)"),
                                                    onehot32[b][:, t // 2, t % 2, :], start=(t == 0), stop=(t == CT - 1))
                    last.then_inc(slots_ps, 1)

                def count_lanes(c, b):
                    te.wait_ge(onehot_ready, c + 1)
                    wait(te, before_ready, c - 1)
                    for t in range(CT):
                        last = nc.tensor.matmul(ps_before[b], before16[:], onehot[b][:, t // 2, :, t % 2],
                                                start=(t == 0), stop=(t == CT - 1))
                    last.then_inc(before_ps, 1)

                count_lanes(0, 0)

                def body(c, b, half):
                    te.wait_ge(before_ready, c + 1)
                    for g in range(NG):
                        wait(te, top_act, c * NG + g - 1)
                        n = len(group(g)) * 2
                        out = ps_count[(b * NG + g) % 2][:, 0:n, :]
                        nc.tensor.matmul(out, unit16[:], across(lanes_before[b][:], n), start=True, stop=False)
                        nc.tensor.matmul(out, lift[:], onehot[b][:, group(g)[0]:group(g)[-1] + 1, :, :]
                                         .rearrange("p g s k -> p g k s"), start=False, stop=True).then_inc(count_ps, 1)
                    if more_after(c):
                        count_lanes(c + 1, 1 - b)
                    if past(c, 1):
                        place(c - 1, 1 - b)

                in_pairs(te, C - 1, body)
                body(C - 1, (C - 1) % 2, (C - 1) // 2)
                place(C - 1, (C - 1) % 2)

            @block.scalar
            def _(act):
                def keep(c, b, half):
                    act.wait_ge(slots_ps, c + 1)
                    lanes = slice(b * SLOTS, b * SLOTS + SLOTS)
                    plain(nc.scalar.activation(at_slot[lanes, :, bass.ds(half, 1)].rearrange("p s o -> p (s o)"),
                                               ps_slots[b][0:SLOTS, :], ACT.Copy)).then_inc(slots_kept, 1)
                    plain(nc.scalar.activation(attr_slot[lanes, :, bass.ds(half, 1)].rearrange("p s o -> p (s o)"),
                                               ps_slots[b][SLOTS:2 * SLOTS, :], ACT.Copy)).then_inc(slots_kept, 1)

                act.wait_ge(mats, 4)

                def take_before(c, b):
                    act.wait_ge(before_ps, c + 1)
                    wait(act, count_ps, (c - 1) * NG)
                    wait(act, top_ready, c - 1)
                    nc.scalar.activation(lanes_before[b][:], ps_before[b], ACT.Copy).then_inc(before_ready, 1)

                take_before(0, 0)

                def body(c, b, half):
                    wait(act, rank_ready, c - 1)
                    for g in range(NG):
                        act.wait_ge(count_ps, c * NG + g + 1)
                        wait(act, top_act, c * NG)
                        for k in range(2 * len(group(g))):
                            t = 2 * group(g)[0] + k
                            last = nc.scalar.activation(ps_count[(b * NG + g) % 2][:, k, :], ps_count[(b * NG + g) % 2][:, k, :], ACT.Relu,
                                                        bias=below_big[:, 0:1], accum_out=top[b][:, t:t + 1])
                        last.then_inc(top_act, 1)
                    if more_after(c):
                        take_before(c + 1, 1 - b)
                    wait(act, slots_ps, c - 1)
                    nc.scalar.activation(onehot32[b][:], onehot[b][:].rearrange("p g s k -> p g k s"),
                                         ACT.Copy).then_inc(onehot32_ready, 1)
                    if past(c, 1):
                        keep(c - 1, 1 - b, half - 1 + b)

                in_pairs(act, C - 1, body)
                body(C - 1, (C - 1) % 2, (C - 1) // 2)
                keep(C - 1, (C - 1) % 2, (C - 1) // 2)

            @block.gpsimd
            def _(pool):
                def body(c, b, half):
                    pool.wait_ge(slot_ready, c + 1)
                    wait(pool, slots_ps, c - 1)
                    for p0, p1 in PIECES:
                        if p1 < TP:
                            plain(nc.gpsimd.tensor_tensor(*product(c, b, p0, p1, 0), ALU.mult)).then_inc(placed_ready, 1)
                        plain(nc.gpsimd.tensor_tensor(*product(c, b, p0, p1, 1), ALU.mult)).then_inc(placed_ready, 1)

                in_pairs(pool, C, body)

            @block.vector
            def _(dve):
                nc.vector.tensor_scalar(lift[:], ident[:], BIG, None, ALU.mult).then_inc(mats, 1)
                nc.vector.tensor_copy(unit16[:], ident[:]).then_inc(mats, 1)
                nc.vector.tensor_copy(before16[:], later[:]).then_inc(mats, 1)
                nc.vector.memset(below_big[:], -BIG).then_inc(mats, 1)
                nc.vector.memset(rank[0][:], -1.0).then_inc(made, 1)
                nc.vector.memset(rank[1][:], -1.0).then_inc(made, 1)
                nc.vector.tensor_copy(iota_slots[:], along(iota[:, 0:SLOTS], 2)).then_inc(made, 1)
                nc.vector.tensor_copy(iota_tiles[:], along(iota[:, 0:NT], 2)).then_inc(made, 1)
                dve.wait_ge(made, 4)

                def hot(c, b):
                    wait(dve, count_ps, (c - 1) * NG)
                    wait(dve, top_ready, c - 1)
                    wait(dve, onehot32_ready, c - 1)
                    nc.vector.tensor_tensor(onehot[b][:],
                                            iota_tiles[:].rearrange("p (o s) k -> p o s k", o=1).broadcast_to([P, TP, NT, 2]),
                                            tile_e[:, bass.ds(c, 1), :].rearrange("p (o s) (g k) -> p (o g) s k", s=1, k=2)
                                            .broadcast_to([P, TP, NT, 2]), ALU.is_equal).then_inc(onehot_ready, 1)

                def ranks(c, b):
                    dve.wait_ge(onehot_ready, c + 1)
                    dve.wait_ge(before_ready, c + 1)
                    for k, t in enumerate(t for t in range(CT) if not R0 <= t < R1):
                        last = nc.vector.scalar_tensor_tensor(out=unused[:, k, :], in0=onehot[b][:, t // 2, :, t % 2],
                                                              scalar=1.0, in1=lanes_before[b][:], op0=ALU.mult,
                                                              op1=ALU.mult, accum_out=top[b][:, t:t + 1])
                    last.then_inc(top_ready, 1)

                def slots(c, b):
                    dve.wait_ge(top_ready, c + 1)
                    dve.wait_ge(top_act, (c + 1) * NG)
                    wait(dve, slot_ready, c - 1)
                    nc.vector.tensor_tensor(rank[b][:, 0:CT], top[b][:], twins[:, bass.ds(c, 1), :].rearrange("p o t -> p (o t)"),
                                            ALU.add).then_inc(rank_ready, 1)
                    dve.wait_ge(rank_ready, c + 1)
                    wait(dve, placed_ready, BY_POOL * (c - 1))
                    nc.vector.tensor_tensor(slot1[b][:],
                                            iota_slots[:].rearrange("p (o s) k -> p o s k", o=1).broadcast_to([P, TP, SLOTS, 2]),
                                            rank[b][:].rearrange("p (g s k) -> p g s k", s=1, k=2).broadcast_to([P, TP, SLOTS, 2]),
                                            ALU.is_equal).then_inc(slot_ready, 1)
                    dve.wait_ge(slot_ready, c + 1)
                    wait(dve, slots_ps, c - 1)
                    nc.vector.tensor_tensor(*product(c, b, *PIECES[-1], 0), ALU.mult).then_inc(last_codes, 1)
                    wait(dve, worst_ready, c)
                    nc.vector.tensor_tensor(worst[:], worst[:], rank[b][:, 0:CT], ALU.max).then_inc(worst_ready, 1)

                hot(0, 0)

                def body(c, b, half):
                    if more_after(c):
                        hot(c + 1, 1 - b)
                    ranks(c, b)
                    slots(c, b)

                in_pairs(dve, C - 1, body)
                body(C - 1, (C - 1) % 2, (C - 1) // 2)
                dve.wait_ge(worst_ready, C)

        check_ready = sem("check_ready")
        check_ps = sem("check_ps")
        check = sb("check", [P, 3], scope=loop_scope)
        over = sb("over", [3, 4], scope=loop_scope)
        dve_check = sem("dve_check")
        over_ready = sem("over_ready")
        over_ps = sem("over_ps")
        with nc.Block() as block:
            @block.tensor
            def _(te):
                te.wait_ge(check_ready, 1)
                nc.tensor.transpose(ps_check[0:3, 0:P], check[:], ident[:]).then_inc(check_ps, 1)
                te.wait_ge(over_ready, 1)
                nc.tensor.matmul(ps_check[0:1, P:P + 1], over[:, 3:4], ones[0:3, 0:1], start=True, stop=True).then_inc(over_ps, 1)

            @block.vector
            def _(dve):
                step = Chain(dve, dve_check)
                step(nc.vector.tensor_reduce(check[:, 0:1], worst[:], AX.X, ALU.max))
                step(nc.vector.tensor_scalar(check[:, 0:1], check[:, 0:1], float(SLOTS - 1), None, ALU.subtract))
                step(nc.vector.tensor_scalar(check[:, 1:2], stray[:, 0:1], float(P - 1), None, ALU.subtract))
                nc.vector.tensor_scalar(check[:, 2:3], stray[:, 1:2], -1.0, None, ALU.mult).then_inc(check_ready, 1)
                dve.wait_ge(check_ps, 1)
                step(nc.vector.tensor_reduce(over[:, 2:3], ps_check[0:3, 0:P], AX.X, ALU.max))
                nc.vector.tensor_scalar(over[:, 3:4], over[:, 2:3], 0.0, None, ALU.is_gt).then_inc(over_ready, 1)
                dve.wait_ge(over_ps, 1)
                step(nc.vector.tensor_scalar(misfit[:], ps_check[0:1, P:P + 1], 1.0, None, ALU.min))
        loop_scope.close()

        windows_scope = ctx.enter_context(ExitStack())
        rows_next = sb("rows_next", [P, C, 2 * H], F16, scope=windows_scope)
        rows_of = (rows_now, rows_next)
        slot_scope = windows_scope.enter_context(ExitStack())
        dst_i16 = sb("dst_i16", [P, NT, JP], I16, scope=slot_scope)
        src_i16 = sb("src_i16", [P, NT, JP], I16, scope=slot_scope)
        dst_lane = sb("dst_lane", [P, J, NT], scope=slot_scope)
        lanes_T = [sb(f"lanes_T{b}", [NT, UJ * P], F16, scope=slot_scope) for b in pair]
        ps_lanes = [ps(f"ps_lanes{b}", [P, UJ * P], scope=slot_scope) for b in pair]
        unpacked = sem("unpacked")
        lanes_ps = sem("lanes_ps")
        lanes_ready = sem("lanes_ready")
        lanes_out = [sem(f"lanes_out{b}") for b in pair]
        dve_unpack = sem("dve_unpack")
        with nc.Block() as block:
            @block.vector
            def _(dve):
                step = Chain(dve, dve_unpack)
                step(nc.vector.tensor_scalar(at_slot[:], at_slot[:], -1.0, None, ALU.add))
                step(nc.vector.tensor_scalar(dst_i16[:].bitcast(I32), at_slot[:].bitcast(I32), (P - 1) * 0x10001, None,
                                             ALU.bitwise_and))
                nc.vector.tensor_copy(dst_lane[:], dst_i16[:, :, 0:J].rearrange("p s j -> p j s")).then_inc(unpacked, 1)
                step(nc.vector.tensor_scalar(src_i16[:].bitcast(I32), at_slot[:].bitcast(I32), 7, 0x1ff * 0x10001,
                                             ALU.arith_shift_right, ALU.bitwise_and))
                step(nc.vector.tensor_copy(src_lane, src_i16[:]))

            @block.tensor
            def _(te):
                te.wait_ge(unpacked, 1)
                for u in range(NU):
                    wait(te, lanes_ready, u - 1)
                    for k, j in enumerate(pairs_of(u)):
                        last = nc.tensor.transpose(ps_lanes[u % 2][0:NT, k * P:(k + 1) * P], dst_lane[:, j, :], ident[:])
                    last.then_inc(lanes_ps, 1)

            @block.scalar
            def _(act):
                for u in range(NU):
                    act.wait_ge(lanes_ps, u + 1)
                    wait(act, lanes_out[u % 2], 16 * (u // 2))
                    n = len(pairs_of(u)) * P
                    nc.scalar.activation(lanes_T[u % 2][:, 0:n], ps_lanes[u % 2][0:NT, 0:n], ACT.Copy).then_inc(lanes_ready, 1)

            @block.sync
            def _(sp):
                for u in range(NU):
                    n = len(pairs_of(u)) * P
                    sp.wait_ge(lanes_ready, u + 1)
                    sp.dma_start(lanes_dram[:, u * UJ * P:u * UJ * P + n], lanes_T[u % 2][:, 0:n]).then_inc(lanes_out[u % 2], 16)
                for b in pair:
                    wait(sp, lanes_out[b], 16 * ((NU + 1 - b) // 2))
        slot_scope.close()

        def only(bind, path):
            def bound(program):
                @bind
                def _(engine):
                    taken = engine.value_load(misfit[0:1, 0:1], min_val=0, max_val=1)
                    with engine.If(taken < 1 if path == TENSOR_PATH else taken > 0):
                        program(engine)
            return bound

        def sums_round(r, scope):
            hcur, sumT, hT, gi, rz, tn, cand = gru_buffers(scope)
            lanes = [sb(f"lanes{q}", [P, QC * SLOTS], F16, scope=scope) for q in range(NQ)]
            dst1 = [sb(f"dst1{q}", [P, QC * SLOTS], F16, scope=scope) for q in range(NQ)]
            src1 = [sb(f"src1{q}", [P, UQ, P, UJ], F16, scope=scope) for q in range(NQ)]
            rows = [sb(f"rows{b}", [P, UJ, 2 * H], F16, scope=scope) for b in range(4)]
            x_rows = attr_slot[:].rearrange("p s j -> p (s j)")[:, 0:NT * H].rearrange("p (t f) -> p t f", t=NT)
            out_rows = [sb(f"out_rows{b}", [P, H], scope=scope) for b in range(2)]
            new_parts = [sb(f"new_parts{b}", [P, 2 * H], F16, scope=scope) for b in range(2)]
            new_rest = sb("new_rest", [P, H], scope=scope)
            attr_left = [sb(f"attr_left{b}", [P, J], scope=scope) for b in range(2)]
            attr_parts = [sb(f"attr_parts{b}", [P, J, 4], BF16, scope=scope) for b in range(2)]
            ps_rows = [ps(f"ps_rows{b}", [P, 512], scope=scope) for b in range(4)]
            iota_units = sb("iota_units", [P, P, UJ], F16, scope=scope)
            nothing = sb("nothing", [P, P], F16, scope=scope)
            sums4 = [sb(f"sums4{b}", [P, 4], scope=scope) for b in range(2)]
            ps_sum = [ps(f"ps_sum{b}", [P, 512], scope=scope) for b in range(2)]
            ps_T = ps("ps_T2", [P, 512], scope=scope)
            ps_gates = ps("ps_gates", [P, 512], scope=scope)

            names = ("rows_zero", "dst1_ready", "src1_ready", "gathered", "rows_ready", "scattered", "parts_ready",
                     "sum_ready", "sums4_ready", "attr_sum", "cur_ready", "turned", "hT_ready", "gates_ready", "gi_half", "gi_ready",
                     "rz_ready", "tn_half", "tn_ready", "cand_ready", "mixed", "h_new", "pool_own")
            (rows_zero, dst1_ready, src1_ready, gathered, rows_ready, scattered, parts_ready,
             sum_ready, sums4_ready, attr_sum, cur_ready, turned, hT_ready, gates_ready, gi_half, gi_ready,
             rz_ready, tn_half, tn_ready, cand_ready, mixed, h_new, pool_own) = [path_sem(f"{n}_{r}") for n in names]
            lanes_in = [path_sem(f"lanes_in{r}_{q}") for q in range(NQ)]
            new_own = path_sem(f"new_own{r}")
            new_low = path_sem(f"new_low{r}")
            new_stored = path_sem(f"new_stored{r}")
            next_in = path_sem(f"next_in{r}")
            iota_ready = path_sem(f"iota_ready{r}")
            x_in = path_sem(f"x_in{r}")
            out_ready = path_sem(f"out_ready{r}")
            out_stored = path_sem(f"out_stored{r}")
            more = r + 1 < ROUNDS

            def fetch_lanes(engine, s):
                for q in range(NQ):
                    wait(engine, dst1_ready, (s - 1) * NQ + q + 1)
                    n = min((q + 1) * QC, 2 * J) - q * QC
                    plain(engine.dma_start(lanes[q][:, 0:n * SLOTS],
                                           lanes_dram[bass.ds(s, 1), q * QC * SLOTS:(q * QC + n) * SLOTS]
                                           .broadcast_to([P, n * SLOTS]))).then_inc(lanes_in[q], 16)

            def done_with(s, q):
                return (s - 1) * NU + units_of(q)[-1] + 1

            with nc.Block() as block:
                @only(block.sync, TENSOR_PATH)
                def _(sp):
                    if not more:
                        def body(s, b, half):
                            fetch_lanes(sp, s)
                            if not past(s, 1):
                                with nc.allow_non_contiguous_dma(reason="rows of nodes"):
                                    sp.dma_start(x_rows[:, 0:NT - 1, :],
                                                 x[0:(NT - 1) * P, :].rearrange("(t p) f -> p t f", p=P)).then_inc(x_in, 16)
                                sp.dma_start(x_rows[0:TAIL, NT - 1, :], x[(NT - 1) * P:N, :]).then_inc(x_in, 16)

                        in_pairs(sp, NT, body)
                        return
                    with sp.Fori(0, C) as c:
                        at = sp.value_load(first[0:1, bass.ds(c, 1)], min_val=0, max_val=NP - P)
                        span = sp.value_load(spans[0:1, bass.ds(c, 1)], min_val=1, max_val=NT)
                        sp.wait_ge(new_stored, 16 * span)
                        sp.dma_start(rows_of[(r + 1) % 2][:, bass.ds(c, 1), :].rearrange("p o f -> p (o f)"),
                                     parts_dram[(r + 1) % 2][bass.ds(at, P), :]).then_inc(next_in, 16)
                    sp.wait_ge(next_in, 16 * C)

                @only(block.gpsimd, TENSOR_PATH)
                def _(pool):
                    def put_out(k, b, half, n=P):
                        pool.wait_ge(h_new, k + 1)
                        wait(pool, out_stored, 16 * k)
                        plain(nc.gpsimd.tensor_tensor(out_rows[b][0:n, :], x_rows[0:n, bass.ds(k, 1), :].rearrange("p o f -> p (o f)"),
                                                      h[0:n, bass.ds(k, 1), 0:H].rearrange("p o f -> p (o f)"),
                                                      ALU.add)).then_inc(out_ready, 1)
                        pool.wait_ge(out_ready, k + 1)
                        plain(pool.dma_start(out[bass.ds(k * P, n), :], out_rows[b][0:n, :])).then_inc(out_stored, 16)

                    if not more:
                        pool.wait_ge(x_in, 32)
                        in_pairs(pool, NT - 1, put_out)
                        put_out(NT - 1, (NT - 1) % 2, 0, TAIL)
                        pool.wait_ge(out_stored, 16 * NT)
                        return

                    def split_attr(s, b):
                        own = lambda n: pool.wait_ge(pool_own, 5 * s + n)
                        wait(pool, scattered, (s - 1) * NU)
                        part = lambda k: attr_parts[b][:, :, k]
                        plain(nc.gpsimd.tensor_copy(attr_left[b][:], attr_slot[:, bass.ds(s, 1), 0:J]
                                                    .rearrange("p o j -> p (o j)"))).then_inc(pool_own, 1)
                        nc.gpsimd.memset(part(3), 1.0).then_inc(parts_ready, 1)
                        own(1)
                        plain(nc.gpsimd.tensor_copy(part(0), attr_left[b][:])).then_inc(pool_own, 1)
                        own(2)
                        nc.gpsimd.tensor_tensor(attr_left[b][:], attr_left[b][:], part(0), ALU.subtract).then_inc(pool_own, 1)
                        own(3)
                        plain(nc.gpsimd.tensor_copy(part(1), attr_left[b][:])).then_inc(pool_own, 1)
                        own(4)
                        nc.gpsimd.tensor_tensor(attr_left[b][:], attr_left[b][:], part(1), ALU.subtract).then_inc(pool_own, 1)
                        own(5)
                        plain(nc.gpsimd.tensor_copy(part(2), attr_left[b][:])).then_inc(parts_ready, 1)

                    def store_rows(k, b):
                        pool.wait_ge(h_new, k + 1)
                        wait(pool, new_stored, 16 * k)
                        now = h[:, bass.ds(k, 1), 0:H].rearrange("p o f -> p (o f)")
                        plain(nc.gpsimd.tensor_copy(new_parts[b][:, 0:H], now)).then_inc(new_own, 1)
                        pool.wait_ge(new_own, 2 * k + 1)
                        wait(pool, new_low, k)
                        plain(nc.gpsimd.tensor_tensor(new_rest[:], now, new_parts[b][:, 0:H], ALU.subtract)).then_inc(new_own, 1)
                        pool.wait_ge(new_own, 2 * k + 2)
                        plain(nc.gpsimd.tensor_scalar(new_parts[b][:, H:2 * H], new_rest[:], LO, None, ALU.mult)).then_inc(new_low, 1)
                        pool.wait_ge(new_low, k + 1)
                        plain(pool.dma_start(parts_dram[(r + 1) % 2][bass.ds(k * P, P), :], new_parts[b][:])).then_inc(new_stored, 16)

                    if r == 0:
                        split_attr(0, 0)

                    def body(s, b, half):
                        fetch_lanes(pool, s)
                        if past(s, 3):
                            store_rows(s - 3, 1 - b)
                        if r == 0 and not (isinstance(s, int) and s == NT - 1):
                            split_attr(s + 1, 1 - b)

                    in_pairs(pool, NT - 1, body)
                    body(NT - 1, (NT - 1) % 2, (NT - 1) // 2)
                    for k in range(NT - 3, NT):
                        store_rows(k, k % 2)

                @only(block.tensor, TENSOR_PATH)
                def _(te):
                    def gather(s, u):
                        q = u // UQ
                        if u % UQ == 0:
                            te.wait_ge(dst1_ready, s * NQ + q + 1)
                        wait(te, rows_ready, s * NU + u - 3)
                        for k, j in enumerate(pairs_of(u)):
                            for half in range(2):
                                c = 2 * j + half
                                if c < C:
                                    last = nc.tensor.matmul(
                                        ps_rows[u % 4][half * SLOTS:(half + 1) * SLOTS, k * 2 * H:(k + 1) * 2 * H],
                                        dst1[q][:, (c - q * QC) * SLOTS:(c - q * QC + 1) * SLOTS], rows_of[r % 2][:, c, :],
                                        start=True, stop=True)
                        last.then_inc(gathered, 1)

                    def scatter(s, u, b):
                        q = u // UQ
                        te.wait_ge(rows_ready, s * NU + u + 1)
                        if u % UQ == 0:
                            te.wait_ge(src1_ready, s * NQ + q + 1)
                        if u == 0:
                            wait(te, sum_ready, s - 1)
                            if r == 0:
                                wait(te, sums4_ready, s - 1)
                                te.wait_ge(parts_ready, 2 * s + 2)
                                nc.tensor.matmul(ps_sum[b][:, 0:P + 4], nothing[:],
                                                 src1[0].rearrange("p u l k -> p (u l k)")[:, 0:P + 4], start=True, stop=False)
                        for k, j in enumerate(pairs_of(u)):
                            hot = src1[q][:, u - q * UQ, :, k]
                            if r == 0:
                                nc.tensor.matmul(ps_sum[b][:, P:P + 4], hot, attr_parts[b][:, j, :],
                                                 start=False, stop=False)
                            last = nc.tensor.matmul(ps_sum[b][:, 0:P], rows[u % 4][:, k, :], hot,
                                                    start=(j == 0 and r > 0), stop=(j == J - 1))
                        last.then_inc(scattered, 1)

                    def turn(k, b):
                        te.wait_ge(cur_ready, k + 1)
                        wait(te, hT_ready, k)
                        nc.tensor.transpose(ps_T[0:HA, 0:P], hcur[b][:], ident[:]).then_inc(turned, 1)

                    def gates(k, b):
                        te.wait_ge(hT_ready, k + 1)
                        te.wait_ge(sum_ready, k + 1)
                        wait(te, tn_ready, k)
                        nc.tensor.matmul(ps_gates[:, 0:4 * H + G], hT[b][:], w_node[:, r, :], start=True, stop=False)
                        nc.tensor.matmul(ps_gates[:, 0:G], sumT[b][:], w_sum[:, r, :], start=False,
                                         stop=True).then_inc(gates_ready, 1)

                    te.wait_ge(rows_zero, 1)

                    def body(s, b, half):
                        later_tile = past(s, 1)
                        for u in range(NU):
                            gather(s, u)
                            if u >= LAG:
                                scatter(s, u - LAG, b)
                            elif later_tile:
                                scatter(s - 1, NU - LAG + u, 1 - b)
                            if later_tile and u == TURN_AT:
                                turn(s - 1, 1 - b)
                            if later_tile and u == GATES_AT:
                                gates(s - 1, 1 - b)

                    in_pairs(te, NT, body)
                    for u in range(NU - LAG, NU):
                        scatter(NT - 1, u, (NT - 1) % 2)
                    turn(NT - 1, (NT - 1) % 2)
                    gates(NT - 1, (NT - 1) % 2)

                @only(block.scalar, TENSOR_PATH)
                def _(act):
                    def take(s, u):
                        act.wait_ge(gathered, s * NU + u + 1)
                        wait(act, scattered, s * NU + u - 3)
                        n = len(pairs_of(u))
                        cut = lambda t: t.rearrange("p (j f) -> p j f", j=UJ)
                        if u == NU - 1 and C % 2:
                            if n > 1:
                                nc.scalar.activation(rows[u % 4][:, 0:n - 1, :], cut(ps_rows[u % 4][:])[:, 0:n - 1, :], ACT.Copy)
                            nc.scalar.activation(rows[u % 4][0:SLOTS, n - 1, :], cut(ps_rows[u % 4][:])[0:SLOTS, n - 1, :],
                                                 ACT.Copy).then_inc(rows_ready, 1)
                        else:
                            nc.scalar.activation(rows[u % 4][:, 0:n, :], cut(ps_rows[u % 4][:])[:, 0:n, :],
                                                 ACT.Copy).then_inc(rows_ready, 1)

                    def take_sum(k, b):
                        act.wait_ge(scattered, (k + 1) * NU)
                        wait(act, gates_ready, k - 1)
                        nc.scalar.activation(sumT[b][:], ps_sum[b][:, 0:P], ACT.Copy).then_inc(sum_ready, 1)
                        if r == 0:
                            wait(act, attr_sum, 2 * (k - 1))
                            nc.scalar.activation(sums4[b][:], ps_sum[b][:, P:P + 4], ACT.Copy).then_inc(sums4_ready, 1)

                    def take_hT(k, b):
                        act.wait_ge(turned, k + 1)
                        nc.scalar.activation(hT[b][:], ps_T[0:HA, 0:P], ACT.Copy).then_inc(hT_ready, 1)

                    def sigmoids(k, b):
                        act.wait_ge(gi_ready, k + 1)
                        nc.scalar.activation(rz[b][:], gi[b][:, 0:2 * H], ACT.Sigmoid).then_inc(rz_ready, 1)

                    def tanhs(k, b):
                        act.wait_ge(tn_ready, k + 1)
                        nc.scalar.activation(cand[b][:], tn[b][:], ACT.Tanh).then_inc(cand_ready, 1)

                    act.wait_ge(rows_zero, 1)

                    def body(s, b, half):
                        one_back = past(s, 1)
                        for u in range(NU):
                            take(s, u)
                            if one_back and u == SUM_AT:
                                take_sum(s - 1, 1 - b)
                            if one_back and u == TURN_AT + 1:
                                take_hT(s - 1, 1 - b)
                            if one_back and u == SIGMOID_AT:
                                sigmoids(s - 1, 1 - b)
                            if past(s, 2) and u == TANH_AT:
                                tanhs(s - 2, b)

                    in_pairs(act, NT, body)
                    b = (NT - 1) % 2
                    tanhs(NT - 2, 1 - b)
                    take_sum(NT - 1, b)
                    take_hT(NT - 1, b)
                    sigmoids(NT - 1, b)
                    tanhs(NT - 1, b)

                @only(block.vector, TENSOR_PATH)
                def _(dve):
                    def one_hots(s, q):
                        n = min((q + 1) * QC, 2 * J) - q * QC
                        dve.wait_ge(lanes_in[q], 16 * s + 16)
                        wait(dve, gathered, done_with(s, q))
                        nc.vector.tensor_scalar(dst1[q][:, 0:n * SLOTS], lanes[q][:, 0:n * SLOTS], lane_no[:, 0:1], None,
                                                ALU.is_equal).then_inc(dst1_ready, 1)
                        wait(dve, scattered, done_with(s, q))
                        units = units_of(q)
                        nc.vector.tensor_tensor(src1[q][:, 0:len(units)],
                                                iota_units[:].rearrange("p (o l) k -> p o l k", o=1)
                                                .broadcast_to([P, len(units), P, UJ]),
                                                src_lane[:, bass.ds(s, 1), units[0] * UJ:(units[-1] + 1) * UJ]
                                                .rearrange("p (o l) (u k) -> p (o u) l k", l=1, k=UJ)
                                                .broadcast_to([P, len(units), P, UJ]),
                                                ALU.is_equal).then_inc(src1_ready, 1)

                    def current(k, b):
                        if r == 0:
                            dve.wait_ge(sums4_ready, k + 1)
                            plain(nc.vector.tensor_reduce(h[:, bass.ds(k, 1), H:H + 1],
                                                          sums4[b][:, 0:3].rearrange("p (o f) -> p o f", o=1),
                                                          AX.X, ALU.add)).then_inc(attr_sum, 1)
                            plain(nc.vector.tensor_copy(degree[:, bass.ds(k, 1)], sums4[b][:, 3:4])).then_inc(attr_sum, 1)
                            dve.wait_ge(attr_sum, 2 * k + 2)
                        wait(dve, turned, k - 1)
                        plain(nc.vector.tensor_copy(hcur[b][:].rearrange("p (o f) -> p o f", o=1),
                                                    h[:, bass.ds(k, 1), :])).then_inc(cur_ready, 1)

                    def gate_inputs(k, b):
                        dve.wait_ge(gates_ready, k + 1)
                        nc.vector.tensor_copy(gi[b][:], ps_gates[:, 0:G]).then_inc(gi_half, 1)
                        dve.wait_ge(gi_half, k + 1)
                        nc.vector.scalar_tensor_tensor(out=gi[b][:], in0=ps_gates[:, 4 * H:4 * H + G],
                                                       scalar=degree[:, bass.ds(k, 1)], in1=gi[b][:],
                                                       op0=ALU.mult, op1=ALU.add).then_inc(gi_ready, 1)

                    def tanh_inputs(k, b):
                        dve.wait_ge(rz_ready, k + 1)
                        nc.vector.tensor_tensor(tn[b][:], rz[b][:, 0:H], ps_gates[:, G:4 * H], ALU.mult).then_inc(tn_half, 1)
                        dve.wait_ge(tn_half, k + 1)
                        nc.vector.tensor_tensor(tn[b][:], tn[b][:], gi[b][:, 2 * H:G], ALU.add).then_inc(tn_ready, 1)

                    def mix(k, b):
                        dve.wait_ge(cand_ready, k + 1)
                        nc.vector.tensor_tensor(tn[b][:], hcur[b][:, 0:H], cand[b][:], ALU.subtract).then_inc(mixed, 1)
                        dve.wait_ge(mixed, 2 * k + 1)
                        nc.vector.tensor_tensor(tn[b][:], tn[b][:], rz[b][:, H:2 * H], ALU.mult).then_inc(mixed, 1)
                        dve.wait_ge(mixed, 2 * k + 2)
                        nc.vector.tensor_tensor(h[:, bass.ds(k, 1), 0:H], tn[b][:].rearrange("p (o f) -> p o f", o=1),
                                                cand[b][:].rearrange("p (o f) -> p o f", o=1), ALU.add).then_inc(h_new, 1)

                    nc.vector.tensor_copy(iota_units[:], along(iota[:], UJ)).then_inc(iota_ready, 1)
                    dve.wait_ge(iota_ready, 1)
                    nc.vector.memset(nothing[:], 0.0)
                    for k in range(4):
                        ins = nc.vector.memset(rows[k][:], 0.0)
                    ins.then_inc(rows_zero, 1)

                    def body(s, b, half):
                        one_hots(s, 0)
                        if past(s, 2):
                            tanh_inputs(s - 2, b)
                        one_hots(s, 1)
                        if past(s, 2):
                            mix(s - 2, b)
                        if past(s, 1):
                            current(s - 1, 1 - b)
                        one_hots(s, 2)
                        one_hots(s, 3)
                        if past(s, 1):
                            gate_inputs(s - 1, 1 - b)

                    in_pairs(dve, NT, body)
                    b = (NT - 1) % 2
                    tanh_inputs(NT - 2, 1 - b)
                    mix(NT - 2, 1 - b)
                    current(NT - 1, b)
                    gate_inputs(NT - 1, b)
                    tanh_inputs(NT - 1, b)
                    mix(NT - 1, b)
                    dve.wait_ge(h_new, NT)

        def general_round(r, scope):
            src_sb = sb("src_sb", [P, ET], I32, scope=scope)
            dst_sb = sb("dst_sb", [P, ET], I32, scope=scope)
            attr_sb = sb("attr_sb", [P, ET], scope=scope)
            src_now = sb("src_now", [P, 1], I32, scope=scope)
            dst_now = sb("dst_now", [P, 1], I32, scope=scope)
            put_at = sb("put_at", [P, 1], I32, scope=scope)
            srcf = sb("srcf", [P, 1], scope=scope)
            payload = sb("payload", [P, HA], scope=scope)
            before = sb("before", [P, HA], scope=scope)
            after = sb("after", [P, HA], scope=scope)
            same = sb("same", [P, P], scope=scope)
            dup = sb("dup", [P, P], scope=scope)
            ndup = sb("ndup", [P, 1], scope=scope)
            putf = sb("putf", [P, 1], scope=scope)
            sums = [sb(f"sums{b}", [P, HA], scope=scope) for b in range(2)]
            hcur, sumT, hT, gi, rz, tn, cand = gru_buffers(scope)
            ps_a = ps("ps_a", [P, 512], scope=scope)
            ps_b = ps("ps_b", [P, 512], scope=scope)
            ps_T = ps("ps_T", [P, 2 * P], scope=scope)
            ps_gates = [ps(f"ps_gates{b}", [P, 512], scope=scope) for b in range(2)]
            edges_in = path_sem(f"edges_in_{r}")
            stored = path_sem(f"stored_{r}")
            now_ready = path_sem(f"now_ready_{r}")
            h_got = path_sem(f"h_got_{r}")
            before_got = path_sem(f"before_got_{r}")
            srcT_ready = path_sem(f"srcT_ready_{r}")
            put_ready = path_sem(f"put_ready_{r}")
            group_sum = path_sem(f"group_sum_{r}")
            after_ready = path_sem(f"after_ready_{r}")
            put_done = path_sem(f"put_done_{r}")
            dve_edge = path_sem(f"dve_edge_{r}")
            N_OWN = 6

            with nc.Block() as block:
                @only(block.sync, GENERAL_PATH)
                def _(sp):
                    with nc.allow_non_contiguous_dma(reason="rows of nodes"):
                        sp.dma_start(src_sb[:], src.rearrange("(p t) -> p t", p=P)).then_inc(edges_in, 16)
                        sp.dma_start(dst_sb[:], dst.rearrange("(p t) -> p t", p=P)).then_inc(edges_in, 16)
                        sp.dma_start(attr_sb[:], attr.rearrange("(p t) o -> p (t o)", p=P)).then_inc(edges_in, 16)
                        sp.dma_start(h_dram.rearrange("(t p) f -> p t f", p=P), h[:, :, 0:H]).then_inc(stored, 16)
                        sp.dma_start(sums_dram.rearrange("(t p) f -> p t f", p=P),
                                     zeros[:].rearrange("p (o f) -> p o f", o=1).broadcast_to([P, NT, HA])).then_inc(stored, 16)
                    sp.wait_ge(stored, 32)

                @only(block.gpsimd, GENERAL_PATH)
                def _(pool):
                    pool.wait_ge(stored, 32)
                    last_node = pool.to_reg(N - 1)
                    def body(i):
                        pool.wait_ge(now_ready, 3 * i + 3)
                        nc.gpsimd.indirect_dma_start(
                            out=payload[:, 0:H], out_offset=None, in_=h_dram,
                            in_offset=bass.IndirectOffsetOnAxis(ap=dst_now[:], axis=0)).wait_op(stored, 32, 'sem-ge').then_inc(h_got, 16)
                        wait(pool, put_done, 16 * i)
                        nc.gpsimd.indirect_dma_start(
                            out=before[:], out_offset=None, in_=sums_dram,
                            in_offset=bass.IndirectOffsetOnAxis(ap=src_now[:], axis=0)).wait_op(stored, 32, 'sem-ge').then_inc(before_got, 16)
                        pool.wait_ge(put_ready, i + 1)
                        pool.wait_ge(after_ready, i + 1)
                        nc.gpsimd.indirect_dma_start(
                            out=sums_dram, out_offset=bass.IndirectOffsetOnAxis(ap=put_at[:], axis=0),
                            in_=after[:], in_offset=None, bounds_check=last_node, oob_is_err=False).wait_op(stored, 32, 'sem-ge').then_inc(put_done, 16)

                    body(0)
                    with pool.Fori(1, ET) as i:
                        body(i)
                    pool.wait_ge(put_done, 16 * ET)

                @only(block.tensor, GENERAL_PATH)
                def _(te):
                    def body(i):
                        te.wait_ge(now_ready, 3 * i + 3)
                        nc.tensor.transpose(ps_a[:, 0:P], srcf[:].broadcast_to([P, P]), ident[:]).then_inc(srcT_ready, 1)
                        te.wait_ge(put_ready, i + 1)
                        te.wait_ge(h_got, 16 * i + 16)
                        nc.tensor.matmul(ps_b[:, 0:HA], same[:], payload[:], start=True, stop=True).then_inc(group_sum, 1)

                    body(0)
                    with te.Fori(1, ET) as i:
                        body(i)

                @only(block.vector, GENERAL_PATH)
                def _(dve):
                    dve.wait_ge(edges_in, 48)
                    nc.vector.memset(payload[:, HA - 1:HA], 1.0)
                    def body(i):
                        wait(dve, put_done, 16 * i)
                        nc.vector.tensor_copy(dst_now[:], dst_sb[:, bass.ds(i, 1)]).then_inc(now_ready, 1)
                        nc.vector.tensor_copy(src_now[:], src_sb[:, bass.ds(i, 1)])
                        nc.vector.tensor_copy(payload[:, H:H + 1], attr_sb[:, bass.ds(i, 1)]).then_inc(now_ready, 1)
                        nc.vector.tensor_copy(srcf[:], src_sb[:, bass.ds(i, 1)]).then_inc(now_ready, 1)
                        dve.wait_ge(now_ready, 3 * i + 3)
                        dve.wait_ge(srcT_ready, i + 1)
                        nc.vector.tensor_scalar(same[:], ps_a[:, 0:P], srcf[:, 0:1], None, ALU.is_equal).then_inc(dve_edge, 1)
                        dve.wait_ge(dve_edge, N_OWN * i + 1)
                        nc.vector.tensor_tensor(dup[:], same[:], earlier[:], ALU.mult).then_inc(dve_edge, 1)
                        dve.wait_ge(dve_edge, N_OWN * i + 2)
                        nc.vector.tensor_reduce(ndup[:], dup[:], AX.X, ALU.add).then_inc(dve_edge, 1)
                        dve.wait_ge(dve_edge, N_OWN * i + 3)
                        nc.vector.tensor_scalar(ndup[:], ndup[:], 1.0, SKIP, ALU.min, ALU.mult).then_inc(dve_edge, 1)
                        dve.wait_ge(dve_edge, N_OWN * i + 4)
                        nc.vector.tensor_tensor(putf[:], ndup[:], srcf[:], ALU.add).then_inc(dve_edge, 1)
                        dve.wait_ge(dve_edge, N_OWN * i + 5)
                        nc.vector.tensor_copy(put_at[:], putf[:]).then_inc(put_ready, 1)
                        dve.wait_ge(group_sum, i + 1)
                        dve.wait_ge(before_got, 16 * i + 16)
                        nc.vector.tensor_tensor(after[:], before[:], ps_b[:, 0:HA], ALU.add).then_inc(after_ready, 1)
                        nc.vector.tensor_copy(ndup[:], ndup[:]).then_inc(dve_edge, 1)

                    body(0)
                    with dve.Fori(1, ET) as i:
                        body(i)

            sums_got = [path_sem(f"sums_got{r}_{b}") for b in range(2)]
            cur_ready = path_sem(f"cur_ready_{r}")
            T_turned = path_sem(f"turned_{r}")
            T_ready = path_sem(f"hT_ready_{r}")
            gates_ready = path_sem(f"gates_ready_{r}")
            gi_ready = path_sem(f"gi_ready_{r}")
            rz_ready = path_sem(f"rz_ready_{r}")
            tn_ready = path_sem(f"tn_ready_{r}")
            cand_ready = path_sem(f"cand_ready_{r}")
            h_new = path_sem(f"h_new_{r}")
            dve_gru = path_sem(f"dve_gru_{r}")

            with nc.Block() as block:
                @only(block.sync, GENERAL_PATH)
                def _(sp):
                    def body(k, b, half):
                        wait(sp, h_new, 2 * half)
                        sp.dma_start(sums[b][:], sums_dram[bass.ds(k * P, P), :]).then_inc(sums_got[b], 16)

                    in_pairs(sp, NT, body)

                @only(block.tensor, GENERAL_PATH)
                def _(te):
                    def body(k, b, half):
                        te.wait_ge(cur_ready, k + 1)
                        wait(te, T_ready, 2 * k)
                        nc.tensor.transpose(ps_T[0:HA, P:2 * P], hcur[b][:], ident[:])
                        nc.tensor.transpose(ps_T[0:H, 0:P], sums[b][:, 0:H], ident[:]).then_inc(T_turned, 1)
                        te.wait_ge(T_ready, 2 * k + 2)
                        wait(te, h_new, 2 * half)
                        nc.tensor.matmul(ps_gates[b][:, 0:4 * H + G], hT[b][:], w_node[:, r, :], start=True, stop=False)
                        nc.tensor.matmul(ps_gates[b][:, 0:G], sumT[b][0:H, :], w_sum[0:H, r, :], start=False,
                                         stop=True).then_inc(gates_ready, 1)

                    in_pairs(te, NT, body)

                @only(block.scalar, GENERAL_PATH)
                def _(act):
                    def body(k, b, half):
                        act.wait_ge(T_turned, k + 1)
                        wait(act, gates_ready, 2 * half)
                        nc.scalar.activation(sumT[b][0:H, :], ps_T[0:H, 0:P], ACT.Copy).then_inc(T_ready, 1)
                        nc.scalar.activation(hT[b][:], ps_T[0:HA, P:2 * P], ACT.Copy).then_inc(T_ready, 1)
                        act.wait_ge(gi_ready, k + 1)
                        nc.scalar.activation(rz[b][:], gi[b][:, 0:2 * H], ACT.Sigmoid).then_inc(rz_ready, 1)
                        act.wait_ge(tn_ready, k + 1)
                        nc.scalar.activation(cand[b][:], tn[b][:], ACT.Tanh).then_inc(cand_ready, 1)

                    in_pairs(act, NT, body)

                @only(block.vector, GENERAL_PATH)
                def _(dve):
                    def body(k, b, half):
                        own = lambda n: 5 * k + n
                        dve.wait_ge(sums_got[b], 16 * half + 16)
                        nc.vector.tensor_copy(h[:, bass.ds(k, 1), H:H + 1],
                                              sums[b][:, H:H + 1].rearrange("p (o f) -> p o f", o=1)).then_inc(dve_gru, 1)
                        dve.wait_ge(dve_gru, own(1))
                        nc.vector.tensor_copy(hcur[b][:].rearrange("p (o f) -> p o f", o=1),
                                              h[:, bass.ds(k, 1), :]).then_inc(cur_ready, 1)
                        dve.wait_ge(gates_ready, k + 1)
                        nc.vector.tensor_copy(gi[b][:], ps_gates[b][:, 0:G]).then_inc(dve_gru, 1)
                        dve.wait_ge(dve_gru, own(2))
                        nc.vector.scalar_tensor_tensor(out=gi[b][:], in0=ps_gates[b][:, 4 * H:4 * H + G],
                                                       scalar=sums[b][:, H + 1:HA], in1=gi[b][:],
                                                       op0=ALU.mult, op1=ALU.add).then_inc(gi_ready, 1)
                        dve.wait_ge(gi_ready, k + 1)
                        dve.wait_ge(rz_ready, k + 1)
                        nc.vector.tensor_tensor(tn[b][:], rz[b][:, 0:H], ps_gates[b][:, G:4 * H], ALU.mult).then_inc(dve_gru, 1)
                        dve.wait_ge(dve_gru, own(3))
                        nc.vector.tensor_tensor(tn[b][:], tn[b][:], gi[b][:, 2 * H:G], ALU.add).then_inc(tn_ready, 1)
                        dve.wait_ge(cand_ready, k + 1)
                        dve.wait_ge(cur_ready, k + 1)
                        nc.vector.tensor_tensor(tn[b][:], hcur[b][:, 0:H], cand[b][:], ALU.subtract).then_inc(dve_gru, 1)
                        dve.wait_ge(dve_gru, own(4))
                        nc.vector.tensor_tensor(tn[b][:], tn[b][:], rz[b][:, H:2 * H], ALU.mult).then_inc(dve_gru, 1)
                        dve.wait_ge(dve_gru, own(5))
                        nc.vector.tensor_tensor(h[:, bass.ds(k, 1), 0:H], tn[b][:].rearrange("p (o f) -> p o f", o=1),
                                                cand[b][:].rearrange("p (o f) -> p o f", o=1), ALU.add).then_inc(h_new, 1)

                    in_pairs(dve, NT, body)


        for r in range(ROUNDS):
            with ExitStack() as scope:
                sums_round(r, scope)
        windows_scope.close()
        for r in range(ROUNDS):
            with ExitStack() as scope:
                general_round(r, scope)

        x_again = sem("x_again")
        added = sem("added")
        result = sem("result")
        wide = sb("wide_again", [P, NT, H])
        with nc.Block() as block:
            @only(block.sync, GENERAL_PATH)
            def _(sp):
                with nc.allow_non_contiguous_dma(reason="rows of nodes"):
                    sp.dma_start(wide[:, 0:NT - 1, :], x[0:(NT - 1) * P, :].rearrange("(t p) f -> p t f", p=P)).then_inc(x_again, 16)
                    sp.dma_start(wide[0:TAIL, NT - 1, :], x[(NT - 1) * P:N, :]).then_inc(x_again, 16)
                    sp.wait_ge(added, 2)
                    sp.dma_start(out[0:(NT - 1) * P, :].rearrange("(t p) f -> p t f", p=P), wide[:, 0:NT - 1, :]).then_inc(result, 16)
                    sp.dma_start(out[(NT - 1) * P:N, :], wide[0:TAIL, NT - 1, :]).then_inc(result, 16)
                sp.wait_ge(result, 32)

            @only(block.vector, GENERAL_PATH)
            def _(dve):
                dve.wait_ge(x_again, 32)
                nc.vector.tensor_tensor(wide[:, 0:NT - 1, :], wide[:, 0:NT - 1, :], h[:, 0:NT - 1, 0:H], ALU.add).then_inc(added, 1)
                nc.vector.tensor_tensor(wide[0:TAIL, NT - 1, :], wide[0:TAIL, NT - 1, :], h[0:TAIL, NT - 1, 0:H],
                                        ALU.add).then_inc(added, 1)


_INS = ["x", "src", "dst", "edge_weight1", "L0_gnn_msg_W", "L0_gnn_msg_b", "L0_gnn_gru_Wih", "L0_gnn_gru_bih",
        "L0_gnn_gru_Whh", "L0_gnn_gru_bhh"]


def kernel(**inputs):
    import numpy as _np
    import concourse.bacc as _bacc
    from concourse import mybir as _mybir
    from concourse.bass_utils import run_bass_kernel_spmd as _run

    nc = _bacc.Bacc("TRN2", target_bir_lowering=False, num_devices=1)
    arrays, args = {}, []
    for name in _INS:
        a = _np.ascontiguousarray(inputs[name])
        arrays[f"in_{name}_dram"] = a
        args.append(nc.dram_tensor(f"in_{name}_dram", a.shape, _mybir.dt.from_np(a.dtype), kind="ExternalInput").ap())
    out = nc.dram_tensor("out_0_dram", inputs["x"].shape, F32, kind="ExternalOutput").ap()
    build(nc, *args, out)
    r = _run(nc, [arrays], core_ids=[0])
    return r.results[0]["out_0_dram"]
```
